# Optimizing a Trainium2 kernel written in Bass

```python
import numpy as np
import jax
import jax.numpy as jnp

def _softmax(x, axis=-1):
    return jax.nn.softmax(x, axis=axis)

def _gelu(x):
    return jax.nn.gelu(x, approximate=True)

def _silu(x):
    return jax.nn.silu(x)

def _sigmoid(x):
    return jax.nn.sigmoid(x)

def _layernorm(x, axis=-1, eps=1e-05):
    m = jnp.mean(x, axis=axis, keepdims=True)
    v = jnp.var(x, axis=axis, keepdims=True)
    return (x - m) / jnp.sqrt(v + eps)

def _scatter_add(tgt, idx, src, axis=0):
    return tgt.at[idx].add(src)

def _segment_sum(src, seg, n):
    return jax.ops.segment_sum(src, seg, n)
kernel_name = 'mk_gnn_preln_d2_gnn_r32_7f6f82'

def setup_inputs(seed: int=0):
    np.random.seed(seed)
    _w = jnp.asarray

    def _rec_inputs():
        import jax
        import jax.numpy as jnp
        _gk = jax.random.key(seed)
        x = -0.0003713 + 1 * jax.random.normal(jax.random.fold_in(_gk, 1), (3125, 256), jnp.float32)
        _s = jax.random.randint(jax.random.fold_in(_gk, 2), (25000,), 0, 3125, jnp.int32)
        _d = jax.random.randint(jax.random.fold_in(_gk, 3), (25000,), 0, 3125, jnp.int32)
        _loop = jnp.arange(3125, dtype=jnp.int32)
        src = jnp.concatenate([_s, _d, _loop])
        dst = jnp.concatenate([_d, _s, _loop])
        _o = jnp.argsort(dst, stable=True)
        src = src[_o]
        dst = dst[_o]
        edge_weight1 = jax.random.uniform(jax.random.fold_in(_gk, 12), (53125, 1), jnp.float32, 0.0, 0.999994)
        return (x, src, dst, edge_weight1)
    x, src, dst, edge_weight1 = _rec_inputs()

    def _L0_gnn_setup():
        import jax, jax.numpy as jnp
        import numpy as np
        N = 50000
        E = 25000
        F = 256
        H = 4
        D = 64
        key = jax.random.key(seed)
        ks = jax.random.split(key, 10)
        s = 0.02
        HD = H * D
        return {'feat': jax.random.normal(ks[0], (N, F), jnp.float32), 'src': jax.random.randint(ks[1], (E,), 0, N), 'dst': jax.random.randint(ks[2], (E,), 0, N), 'Wq': jax.random.normal(ks[3], (HD, F), jnp.float32) * s, 'bq': jnp.zeros((HD,), jnp.float32), 'Wk': jax.random.normal(ks[4], (HD, F), jnp.float32) * s, 'bk': jnp.zeros((HD,), jnp.float32), 'Wv': jax.random.normal(ks[5], (HD, F), jnp.float32) * s, 'bv': jnp.zeros((HD,), jnp.float32), 'Wskip': jax.random.normal(ks[6], (HD, F), jnp.float32) * s, 'bskip': jnp.zeros((HD,), jnp.float32), 'Wgate': jax.random.normal(ks[7], (1, 3 * HD), jnp.float32) * s, 'bgate': jnp.zeros((1,), jnp.float32), 'ln_w': jnp.ones((HD,), jnp.float32), 'ln_b': jnp.zeros((HD,), jnp.float32), 'prelu_a': jnp.float32(0.25)}
    _L0_gnn_all = _L0_gnn_setup()
    _L0_gnn_in = {k: v for k, v in _L0_gnn_all.items() if k in ('Wq', 'bq', 'Wk', 'bk', 'Wv', 'bv', 'Wskip', 'bskip', 'Wgate', 'bgate', 'ln_w', 'ln_b', 'prelu_a')}
    del _L0_gnn_all

    def _L1_gnn_setup():
        import jax, jax.numpy as jnp
        import numpy as np
        N_NODES = 10000
        N_EDGES = 10000
        D_IN = 256
        D_OUT = 256
        key = jax.random.key(seed)
        k1, k2, k3, k4, k5, k6 = jax.random.split(key, 6)
        feat = jax.random.normal(k1, (N_NODES, D_IN), dtype=jnp.float32)
        eweight = jax.random.uniform(k2, (N_EDGES, 1), dtype=jnp.float32)
        W = jax.random.normal(k3, (D_OUT, 2 * D_IN), dtype=jnp.float32) / np.sqrt(2 * D_IN)
        b = jax.random.normal(k4, (D_OUT,), dtype=jnp.float32) * 0.01
        src = jax.random.randint(k5, (N_EDGES,), 0, N_NODES, dtype=jnp.int64)
        dst = jax.random.randint(k6, (N_EDGES,), 0, N_NODES, dtype=jnp.int64)
        return {'feat': feat, 'eweight': eweight, 'W': W, 'b': b, 'src': src, 'dst': dst}
    _L1_gnn_all = _L1_gnn_setup()
    _L1_gnn_in = {k: v for k, v in _L1_gnn_all.items() if k in ('W', 'b')}
    del _L1_gnn_all
    return {'x': x, 'src': src, 'dst': dst, 'edge_weight1': edge_weight1, 'L0_gnn_Wq': _L0_gnn_in['Wq'], 'L0_gnn_bq': _L0_gnn_in['bq'], 'L0_gnn_Wk': _L0_gnn_in['Wk'], 'L0_gnn_bk': _L0_gnn_in['bk'], 'L0_gnn_Wv': _L0_gnn_in['Wv'], 'L0_gnn_bv': _L0_gnn_in['bv'], 'L0_gnn_Wskip': _L0_gnn_in['Wskip'], 'L0_gnn_bskip': _L0_gnn_in['bskip'], 'L0_gnn_Wgate': _L0_gnn_in['Wgate'], 'L0_gnn_bgate': _L0_gnn_in['bgate'], 'L0_gnn_ln_w': _L0_gnn_in['ln_w'], 'L0_gnn_ln_b': _L0_gnn_in['ln_b'], 'L0_gnn_prelu_a': _L0_gnn_in['prelu_a'], 'L1_gnn_W': _L1_gnn_in['W'], 'L1_gnn_b': _L1_gnn_in['b']}

def reference(x, src, dst, edge_weight1, L0_gnn_Wq, L0_gnn_bq, L0_gnn_Wk, L0_gnn_bk, L0_gnn_Wv, L0_gnn_bv, L0_gnn_Wskip, L0_gnn_bskip, L0_gnn_Wgate, L0_gnn_bgate, L0_gnn_ln_w, L0_gnn_ln_b, L0_gnn_prelu_a, L1_gnn_W, L1_gnn_b):
    import jax
    import jax.numpy as jnp

    def _L0_gnn_ref(feat, src, dst, Wq, bq, Wk, bk, Wv, bv, Wskip, bskip, Wgate, bgate, ln_w, ln_b, prelu_a):
        import jax, jax.numpy as jnp
        import numpy as np
        N = 50000
        E = 25000
        F = 256
        H = 4
        D = 64
        n = feat.shape[0]
        scale = 1.0 / np.sqrt(D).astype(np.float32)
        q = (feat @ Wq.T + bq).reshape(n, H, D)
        k = (feat @ Wk.T + bk).reshape(n, H, D)
        v = (feat @ Wv.T + bv).reshape(n, H, D)
        e = jnp.einsum('ehd,ehd->eh', q[src], k[dst]) * scale
        m = jax.ops.segment_max(e, dst, num_segments=n)
        ex = jnp.exp(e - m[dst])
        denom = jax.ops.segment_sum(ex, dst, num_segments=n)
        sa = ex / denom[dst]
        agg = jax.ops.segment_sum(sa[:, :, None] * v[src], dst, num_segments=n)
        rst = agg.reshape(n, H * D)
        skip = feat @ Wskip.T + bskip
        g = jax.nn.sigmoid(jnp.concatenate([skip, rst, skip - rst], axis=-1) @ Wgate.T + bgate)
        rst = g * skip + (1.0 - g) * rst
        mu = rst.mean(-1, keepdims=True)
        var = rst.var(-1, keepdims=True)
        rst = (rst - mu) * jax.lax.rsqrt(var + 1e-05) * ln_w + ln_b
        return jnp.where(rst >= 0, rst, prelu_a * rst)

    def _L1_gnn_ref(feat, eweight, W, b, src, dst):
        import jax, jax.numpy as jnp
        import numpy as np
        N_NODES = 10000
        N_EDGES = 10000
        D_IN = 256
        D_OUT = 256
        n = feat.shape[0]
        msg = feat[src] * eweight
        agg = jax.ops.segment_sum(msg, dst, num_segments=n)
        deg = jax.ops.segment_sum(jnp.ones((src.shape[0],), dtype=feat.dtype), dst, num_segments=n)
        h_neigh = agg / jnp.maximum(deg, 1.0)[:, None]
        h = jnp.concatenate([h_neigh, feat], axis=-1)
        return h @ W.T + b
    h = jnp.maximum(_layernorm(x, axis=-1), 0.0)
    x = x + _L0_gnn_ref(h, src, dst, L0_gnn_Wq, L0_gnn_bq, L0_gnn_Wk, L0_gnn_bk, L0_gnn_Wv, L0_gnn_bv, L0_gnn_Wskip, L0_gnn_bskip, L0_gnn_Wgate, L0_gnn_bgate, L0_gnn_ln_w, L0_gnn_ln_b, L0_gnn_prelu_a)
    h = jnp.maximum(_layernorm(x, axis=-1), 0.0)
    x = x + _L1_gnn_ref(h, edge_weight1, L1_gnn_W, L1_gnn_b, src, dst)
    return x

_drawn_inputs = setup_inputs


def setup_inputs(seed=0):
    import zlib

    import numpy as np

    out = dict(_drawn_inputs(seed))
    spreads = {'L0_gnn_bq': (0.0, 0.8),
     'L0_gnn_bk': (0.0, 0.8),
     'L0_gnn_bv': (0.0, 0.1),
     'L0_gnn_bskip': (0.0, 0.1),
     'L0_gnn_ln_w': (1.0, 0.2),
     'L0_gnn_ln_b': (0.0, 0.1)}
    factors = {'L0_gnn_Wq': 8.0, 'L0_gnn_Wk': 8.0, 'L1_gnn_b': 8.0}
    for name, (base, spread) in spreads.items():
        noise = np.random.default_rng([zlib.crc32(name.encode()), seed]).standard_normal(out[name].shape)
        drawn = base * np.exp(spread * noise) if base else spread * noise
        out[name] = jnp.asarray(drawn.astype(out[name].dtype))
    for name, factor in factors.items():
        out[name] = (out[name] * factor).astype(out[name].dtype)
    return out
```

```python
import concourse.bass as bass
from concourse import mybir
from contextlib import ExitStack

F32 = mybir.dt.float32
BF16 = mybir.dt.bfloat16
I32 = mybir.dt.int32
ALU = mybir.AluOpType
ACT = mybir.ActivationFunctionType
AX = mybir.AxisListType

P = 128
HEADS = 4


def gnn_kernel(nc, x, src, dst, edge_weight, Wq, bq, Wk, bk, Wv, bv, Wskip, bskip, Wgate, bgate,
               ln_w, ln_b, prelu_a, W1, b1, out):
    N, D = x.shape
    E = src.shape[0]
    DH = D // HEADS
    NT = -(-N // P)
    LAST_ROWS = N - (NT - 1) * P
    ET = -(-E // P)
    LAST_EDGES = E - (ET - 1) * P
    STEPS = ET + NT - 1
    U = 8
    ITERS = STEPS // U
    assert STEPS % U == 0
    EC = 4
    ER = ET // EC
    SC = 4
    SR = STEPS // SC
    assert ET % EC == 0 and STEPS % SC == 0 and ER <= P and SR <= P
    LAST_C = (ET - 1) // ER
    LAST_P = (ET - 1) % ER
    NB = 5
    NG = NT // NB
    assert NT % NB == 0
    SCALE = float(DH) ** -0.5
    NEG = -1.0e30
    FAR = 1 << 20
    DEN = D
    DEG = D + HEADS
    AW = D + 8

    q_tab = nc.dram_tensor("q_tab", (NT * P, D), F32, kind="Internal").ap()
    v_tab = nc.dram_tensor("v_tab", (NT * P, D), F32, kind="Internal").ap()
    h_tab = nc.dram_tensor("h_tab", (NT * P, D), F32, kind="Internal").ap()
    local_tab = nc.dram_tensor("local_tab", (STEPS, P), BF16, kind="Internal").ap()

    with ExitStack() as ctx:
        def sb(name, shape, dt=F32):
            return ctx.enter_context(nc.sbuf_tensor(name, shape, dt))

        stage = ExitStack()

        def tb(name, shape, dt=F32):
            return stage.enter_context(nc.sbuf_tensor(name, shape, dt))

        def sem(name):
            return ctx.enter_context(nc.semaphore(name))

        xs = sb("xs", [P, NT, D])
        ks = sb("ks", [P, NT, 2, D])
        acc = sb("acc", [P, NT, AW])
        ring = sb("ring", [P, U, AW])
        wT = sb("wT", [P, 2, 4 * D])
        w1T = sb("w1T", [P, 4, D])
        bias = sb("bias", [P, 4 * D])
        gate = sb("gate", [P, 3 * D])
        gate_u = sb("gate_u", [P, D])
        gate_w = sb("gate_w", [P, D])
        lnw = sb("lnw", [P, D])
        lnb = sb("lnb", [P, D])
        b1s = sb("b1s", [P, D])
        bg = sb("bg", [P, 1])
        pa = sb("pa", [P, 1])
        ident = sb("ident", [P, P])
        ones = sb("ones", [P, P])
        iota_f = sb("iota_f", [P, STEPS])
        t_row = sb("t_row", [P, STEPS])
        t_int = sb("t_int", [1, STEPS], I32)
        v_src = sb("v_src", [P, STEPS + U], I32)
        v_loc = sb("v_loc", [P, STEPS])
        v_wgt = sb("v_wgt", [P, STEPS])
        maskb = sb("maskb", [P, STEPS])
        row_start = sb("row_start", [SR, SC, P])
        src_stage = sb("src_stage", [P, U], I32)
        stats = sb("stats", [P, NT, 6])
        mean = sb("mean", [P, NT])
        rstd = sb("rstd", [P, NT])
        shift = sb("shift", [P, NT])
        t_a = sb("t_a", [P, NT])
        t_b = sb("t_b", [P, NT])
        pcol = sb("pcol", [P, 1])
        score = sb("score", [P, STEPS * HEADS])
        zz = sb("zz", [P, NT])
        rden = sb("rden", [P, NT, HEADS])
        rdeg = sb("rdeg", [P, NT])

        passed = sem("passed")

        bank = [ctx.enter_context(nc.psum_tensor(f"bank{i}", [P, 512], F32)) for i in range(8)]

        class Chain:

            def __init__(self, eng, name):
                self.eng, self.sem, self.n = eng, sem(name), 0

            def follow(self, ins):
                ins.then_inc(self.sem, 1)
                self.n = self.n + 1
                self.eng.wait_ge(self.sem, self.n)

            def pass_wait(self):
                self.eng.sem_inc(passed, 1)

            def enter(self, i, per):
                self.base, self.per = self.n, per
                self.n = i * per + self.base

            def leave(self, count):
                self.n = self.base + self.per * count

        V, A, G, T_ = nc.vector, nc.scalar, nc.gpsimd, nc.tensor

        wnat = tb("wnat", [P, 8, D])
        w1nat = tb("w1nat", [P, 2, 2 * D])
        iota_i = tb("iota_i", [P, STEPS], I32)
        part_i = tb("part_i", [P, EC], I32)
        part_f = tb("part_f", [P, EC])
        step_i = tb("step_i", [P, SC], I32)
        step_f = tb("step_f", [P, SC])
        bound_i = tb("bound_i", [P, NT - 1], I32)
        bound_f = tb("bound_f", [P, NT - 1])
        nt_i = tb("nt_i", [P, NT - 1], I32)
        nt_f = tb("nt_f", [P, NT - 1])
        e_int = tb("e_int", [ER, 2, EC, P], I32)
        e_src = tb("e_src", [ER, EC, P])
        e_dst = tb("e_dst", [ER, EC, P])
        e_wgt = tb("e_wgt", [ER, EC, P])
        e_start = tb("e_start", [ER, EC, P])
        prev_i = tb("prev_i", [ER, EC], I32)
        prev_f = tb("prev_f", [ER, EC])
        below = tb("below", [ER, NT - 1, EC])
        turn = tb("turn", [P, NT - 1])
        reached = tb("reached", [SR, SC, NT - 1])
        tcol = tb("tcol", [SR, SC])
        tcol_bc = tb("tcol_bc", [SR, SC, P])
        r_row = tb("r_row", [P, STEPS])
        sel = tb("sel", [ER, EC, STEPS])
        row_loc = tb("row_loc", [SR, SC, P])
        row_loc_b = tb("row_loc_b", [SR, SC, P], BF16)
        row_in = tb("row_in", [SR, SC, P])
        pcol_i = tb("pcol_i", [P, 1], I32)
        with nc.Block() as block:
            x_zeroed, x_in, small_in = sem("x_zeroed"), sem("x_in"), sem("small_in")
            weights_in, edges_in, edges_padded = sem("weights_in"), sem("edges_in"), sem("edges_padded")
            consts_set, masks_set = sem("consts_set"), sem("masks_set")
            weightsT, below_ready, below_summed = sem("weightsT"), sem("below_ready"), sem("below_summed")
            tcol_ready, trow_summed = sem("tcol_ready"), sem("trow_summed")
            weights_copied = sem("weights_copied")
            sel_ready, picked, local_ready, local_out = sem("sel_ready"), sem("picked"), sem("local_ready"), sem("local_out")

            @block.sync
            def _(sp):
                sp.dma_start(wnat[:, 0:2, :], Wq.rearrange("(b p) d -> p b d", p=P)).then_inc(weights_in, 16)
                sp.dma_start(wnat[:, 2:4, :], Wv.rearrange("(b p) d -> p b d", p=P)).then_inc(weights_in, 16)
                sp.dma_start(wnat[:, 4:6, :], Wk.rearrange("(b p) d -> p b d", p=P)).then_inc(weights_in, 16)
                sp.dma_start(wnat[:, 6:8, :], Wskip.rearrange("(b p) d -> p b d", p=P)).then_inc(weights_in, 16)
                sp.dma_start(w1nat[:, :, :], W1.rearrange("(b p) d -> p b d", p=P)).then_inc(weights_in, 16)
                sp.dma_start(xs[:, 0:NT - 1, :], x[0:(NT - 1) * P, :].rearrange("(t p) d -> p t d", p=P)).then_inc(x_in, 16)
                sp.wait_ge(x_zeroed, 1)
                sp.dma_start(xs[0:LAST_ROWS, NT - 1, :], x[(NT - 1) * P:N, :]).then_inc(x_in, 16)
                for n, vec in enumerate((bq, bv, bk, bskip)):
                    sp.dma_start(bias[:, n * D:(n + 1) * D], vec.partition_broadcast(P)).then_inc(small_in, 16)
                sp.dma_start(gate[:, :], Wgate[0, :].partition_broadcast(P)).then_inc(small_in, 16)
                sp.dma_start(lnw[:, :], ln_w.partition_broadcast(P)).then_inc(small_in, 16)
                sp.dma_start(lnb[:, :], ln_b.partition_broadcast(P)).then_inc(small_in, 16)
                sp.dma_start(b1s[:, :], b1.partition_broadcast(P)).then_inc(small_in, 16)
                sp.dma_start(bg[:, :], bgate.partition_broadcast(P)).then_inc(small_in, 16)
                sp.dma_start(pa[:, :], prelu_a.partition_broadcast(P)).then_inc(small_in, 16)
                sp.wait_ge(local_ready, 1)
                sp.dma_start(local_tab.rearrange("(c r) e -> r c e", r=SR), row_loc_b[:, :, :]).then_inc(local_out, 16)
                sp.wait_ge(local_out, 16)
                sp.wait_ge(small_in, 160)

            @block.gpsimd
            def _(pool):
                G.memset(e_int[:, 0, LAST_C, :], 0).then_inc(edges_padded, 1)
                G.memset(e_int[:, 1, LAST_C, :], FAR).then_inc(edges_padded, 1)
                G.memset(e_wgt[:, LAST_C, :], 0.0).then_inc(edges_padded, 1)
                G.memset(prev_i[:, :], -1).then_inc(edges_padded, 1)
                G.memset(xs[:, NT - 1, :], 0.0).then_inc(x_zeroed, 1)
                G.iota(iota_i[:, :], [[1, STEPS]], base=0, channel_multiplier=0).then_inc(consts_set, 1)
                G.iota(part_i[:, :], [[ER, EC]], base=0, channel_multiplier=1).then_inc(consts_set, 1)
                G.iota(step_i[:, :], [[SR, SC]], base=0, channel_multiplier=1).then_inc(consts_set, 1)
                G.iota(bound_i[:, :], [[P, NT - 1]], base=P, channel_multiplier=0).then_inc(consts_set, 1)
                G.iota(nt_i[:, :], [[1, NT - 1]], base=1, channel_multiplier=0).then_inc(consts_set, 1)
                G.iota(pcol_i[:, :], [[0, 1]], base=0, channel_multiplier=1).then_inc(consts_set, 1)
                G.memset(ones[:, :], 1.0).then_inc(consts_set, 1)
                G.memset(ident[:, :], 0.0).then_inc(masks_set, 1)
                pool.wait_ge(masks_set, 1)
                G.affine_select(out=ident[:, :], in_=ident[:, :], compare_op=ALU.not_equal, fill=1.0,
                                base=0, pattern=[[-1, P]], channel_multiplier=1).then_inc(masks_set, 1)
                G.memset(acc[:, :, :], 0.0)
                G.memset(v_src[:, STEPS:STEPS + U], 0)
                G.memset(ring[:, :, :], 1.0)

            @block.scalar
            def _(act):
                act.wait_ge(edges_padded, 4)
                full = LAST_C * ER * P
                rest = (ET - 1) * P
                for n, arr in enumerate((src, dst)):
                    act.dma_start(e_int[:, n, 0:LAST_C, :], arr[0:full].rearrange("(c r e) -> r c e", r=ER, e=P)).then_inc(edges_in, 16)
                    act.dma_start(e_int[0:LAST_P, n, LAST_C, :], arr[full:rest].rearrange("(r e) -> r e", e=P)).then_inc(edges_in, 16)
                    act.dma_start(e_int[LAST_P:LAST_P + 1, n, LAST_C, 0:LAST_EDGES], arr[rest:E].unsqueeze(0)).then_inc(edges_in, 16)
                last_of = dst[0:rest].rearrange("(k e) -> k e", e=P)[:, P - 1:P]
                act.dma_start(prev_i[1:ER, 0:1], last_of[0:ER - 1, :], allow_slow_non_contiguous=True).then_inc(edges_in, 16)
                for c in range(1, EC):
                    act.dma_start(prev_i[:, c:c + 1], last_of[c * ER - 1:(c + 1) * ER - 1, :], allow_slow_non_contiguous=True).then_inc(edges_in, 16)
                wgt = edge_weight.rearrange("e o -> (e o)")
                act.dma_start(e_wgt[:, 0:LAST_C, :], wgt[0:full].rearrange("(c r e) -> r c e", r=ER, e=P)).then_inc(edges_in, 16)
                act.dma_start(e_wgt[0:LAST_P, LAST_C, :], wgt[full:rest].rearrange("(r e) -> r e", e=P)).then_inc(edges_in, 16)
                act.dma_start(e_wgt[LAST_P:LAST_P + 1, LAST_C, 0:LAST_EDGES], wgt[rest:E].unsqueeze(0)).then_inc(edges_in, 16)
                for c in range(2):
                    for half in range(2):
                        act.wait_ge(weightsT, 2 * c + half + 1)
                        A.copy(wT[:, c, half * 512:(half + 1) * 512], bank[2 * c + half][:, :]).then_inc(weights_copied, 1)
                for k in range(2):
                    act.wait_ge(weightsT, 5 + k)
                    A.copy(w1T[:, 2 * k:2 * k + 2, :], bank[4 + k][:, :].rearrange("p (k d) -> p k d", k=2)).then_inc(weights_copied, 1)
                act.wait_ge(x_in, 32)

            @block.tensor
            def _(pe):
                pe.wait_ge(masks_set, 2)
                pe.wait_ge(weights_in, 80)
                for c in range(2):
                    for half in range(2):
                        for b in range(4):
                            last = T_.transpose(bank[2 * c + half][:, b * P:(b + 1) * P], wnat[:, 4 * half + b, c * P:(c + 1) * P], ident[:, :])
                        last.then_inc(weightsT, 1)
                for k2 in range(2):
                    for k in range(2):
                        for b in range(2):
                            last = T_.transpose(bank[4 + k2][:, (2 * k + b) * P:(2 * k + b + 1) * P],
                                                w1nat[:, b, (2 * k2 + k) * P:(2 * k2 + k + 1) * P], ident[:, :])
                    last.then_inc(weightsT, 1)
                pe.wait_ge(below_ready, 1)
                for c in range(EC):
                    last = T_.matmul(bank[6][:, 0:NT - 1], ones[0:ER, :], below[:, :, c], start=(c == 0), stop=(c == EC - 1))
                last.then_inc(below_summed, 1)
                pe.wait_ge(tcol_ready, 1)
                for c in range(SC):
                    last = T_.matmul(bank[7][:, c * SR:(c + 1) * SR], tcol_bc[:, c, :], ident[0:SR, 0:SR], start=True, stop=True)
                last.then_inc(trow_summed, 1)
                pe.wait_ge(sel_ready, 1)
                pe.wait_ge(weights_copied, 6)
                for n, what in enumerate((e_dst, e_src, e_wgt)):
                    for c in range(EC):
                        last = T_.matmul(bank[n][:, 0:STEPS], what[:, c, :], sel[:, c, :], start=(c == 0), stop=(c == EC - 1))
                for n, what in enumerate((e_dst, e_start)):
                    for sc in range(SC):
                        for c in range(EC):
                            last = T_.matmul(bank[3 + n][0:SR, sc * P:(sc + 1) * P], sel[:, c, sc * SR:(sc + 1) * SR], what[:, c, :],
                                             start=(c == 0), stop=(c == EC - 1))
                last.then_inc(picked, 1)

            @block.vector
            def _(dve):
                chain = Chain(dve, "index_chain")
                f = chain.follow
                dve.wait_ge(consts_set, 7)
                V.tensor_copy(iota_f[:, :], iota_i[:, :])
                V.tensor_copy(part_f[:, :], part_i[:, :])
                V.tensor_copy(step_f[:, :], step_i[:, :])
                V.tensor_copy(bound_f[:, :], bound_i[:, :])
                V.tensor_copy(pcol[:, :], pcol_i[:, :])
                f(V.tensor_copy(nt_f[:, :], nt_i[:, :]))
                dve.wait_ge(edges_in, 13 * 16)
                V.tensor_copy(e_src[:, :, :], e_int[:, 0, :, :])
                V.tensor_copy(e_dst[:, :, :], e_int[:, 1, :, :])
                f(V.tensor_copy(prev_f[:, :], prev_i[:, :]))
                V.tensor_tensor(e_start[:, :, 1:P], e_dst[:, :, 1:P], e_dst[:, :, 0:P - 1], ALU.not_equal)
                V.tensor_tensor(e_start[:, :, 0], e_dst[:, :, 0], prev_f[:, :], ALU.not_equal)
                V.tensor_tensor(below[:, :, :], bound_f[0:ER, :].unsqueeze(2).to_broadcast([ER, NT - 1, EC]),
                                e_dst[:, :, P - 1].unsqueeze(1).to_broadcast([ER, NT - 1, EC]), ALU.is_gt).then_inc(below_ready, 1)
                dve.wait_ge(below_summed, 1)
                f(V.tensor_tensor(turn[:, :], bank[6][:, 0:NT - 1], nt_f[:, :], ALU.add))
                f(V.tensor_tensor(reached[:, :, :], step_f[0:SR, :].unsqueeze(2).to_broadcast([SR, SC, NT - 1]),
                                  turn[0:SR, :].unsqueeze(1).to_broadcast([SR, SC, NT - 1]), ALU.is_ge))
                f(V.tensor_reduce(tcol[:, :], reached[:, :, :], AX.X, ALU.add))
                V.tensor_copy(tcol_bc[:, :, :], tcol[:, :].unsqueeze(2).to_broadcast([SR, SC, P])).then_inc(tcol_ready, 1)
                dve.wait_ge(trow_summed, 1)
                f(V.tensor_copy(t_row[:, :], bank[7][:, 0:STEPS]))
                V.tensor_copy(t_int[:, :], t_row[0:1, :])
                f(V.tensor_tensor(r_row[:, :], iota_f[:, :], t_row[:, :], ALU.subtract))
                for c in range(EC):
                    last = V.tensor_scalar(sel[:, c, :], r_row[0:ER, :], part_f[0:ER, c:c + 1], None, ALU.is_equal)
                last.then_inc(sel_ready, 1)
                dve.wait_ge(picked, 1)
                V.tensor_copy(v_src[:, 0:STEPS], bank[1][:, 0:STEPS])
                V.tensor_copy(v_wgt[:, :], bank[2][:, 0:STEPS])
                f(V.scalar_tensor_tensor(v_loc[:, :], t_row[:, :], float(-P), bank[0][:, 0:STEPS], ALU.mult, ALU.add))
                f(V.tensor_scalar(v_loc[:, :], v_loc[:, :], -1.0, float(P), ALU.max, ALU.min))
                V.tensor_scalar(r_row[:, :], v_loc[:, :], 0.0, NEG, ALU.is_lt, ALU.mult)
                f(V.tensor_scalar(maskb[:, :], v_loc[:, :], float(P), NEG, ALU.is_ge, ALU.mult))
                V.tensor_tensor(maskb[:, :], maskb[:, :], r_row[:, :], ALU.add)
                f(V.tensor_scalar(tcol[:, :], tcol[:, :], float(P), None, ALU.mult))
                for sc in range(SC):
                    last = V.tensor_scalar(row_loc[:, sc, :], bank[3][0:SR, sc * P:(sc + 1) * P], tcol[:, sc:sc + 1], None, ALU.subtract)
                f(last)
                f(V.tensor_scalar(row_loc[:, :, :], row_loc[:, :, :], -1.0, float(P), ALU.max, ALU.min))
                V.tensor_copy(row_loc_b[:, :, :], row_loc[:, :, :]).then_inc(local_ready, 1)
                V.tensor_scalar(row_in[:, :, :], row_loc[:, :, :], 0.0, NEG, ALU.is_ge, ALU.mult)
                f(V.tensor_scalar(row_start[:, :, :], row_loc[:, :, :], float(P), None, ALU.is_lt))
                f(V.tensor_tensor(row_in[:, :, :], row_in[:, :, :], row_start[:, :, :], ALU.mult))
                V.tensor_tensor(row_start[:, :, :], row_in[:, :, :],
                                bank[4][0:SR, :].rearrange("p (c e) -> p c e", c=SC), ALU.mult)

        stage.close()
        h_buf = tb("h_buf", [P, 2, D])
        hT = tb("hT", [P, 2, 2, P])
        qv_out = tb("qv_out", [P, 2, 2 * D])
        def moments(f):
            m0, v0, m1, v1 = stats[:, :, 1], stats[:, :, 2], stats[:, :, 4], stats[:, :, 5]
            V.tensor_tensor(t_a[:, :], m0, m1, ALU.subtract)
            V.tensor_tensor(mean[:, :], m0, m1, ALU.add)
            f(V.tensor_tensor(t_b[:, :], v0, v1, ALU.add))
            f(V.tensor_tensor(t_a[:, :], t_a[:, :], t_a[:, :], ALU.mult))
            V.tensor_scalar(mean[:, :], mean[:, :], 0.5, None, ALU.mult)
            V.tensor_scalar(t_a[:, :], t_a[:, :], 0.25, None, ALU.mult)
            f(V.tensor_scalar(t_b[:, :], t_b[:, :], 1.0 / D, 1e-5, ALU.mult, ALU.add))
            f(V.tensor_tensor(t_b[:, :], t_b[:, :], t_a[:, :], ALU.add))

        def pairs(eng, body):
            with eng.Fori(0, NT // 2) as i:
                body(i * 2, i, 0, False)
                body(i * 2 + 1, i, 1, False)
            body(NT - 1, NT // 2, 0, True)

        with nc.Block() as block:
            var_ready, root_ready, norm_ready = sem("var_ready"), sem("root_ready"), sem("norm_ready")
            h_ready, h_turned, hT_ready = sem("h_ready"), sem("h_turned"), sem("hT_ready")
            proj_done, proj_read, rows_ready = sem("proj_done"), sem("proj_read"), sem("rows_ready")
            rows_stored = [sem("rows_stored0"), sem("rows_stored1")]

            @block.vector
            def _(dve):
                f = Chain(dve, "norm_chain").follow
                with dve.Fori(0, NT) as T:
                    V.bn_stats(stats[:, bass.ds(T, 1), :], xs[:, bass.ds(T, 1), :])
                f(V.tensor_tensor(gate_u[:, :], gate[:, 0:D], gate[:, 2 * D:3 * D], ALU.add))
                moments(f)
                V.tensor_tensor(gate_w[:, :], gate[:, 0:D], gate[:, D:2 * D], ALU.add).then_inc(var_ready, 1)
                dve.wait_ge(root_ready, 1)
                f(V.reciprocal(rstd[:, :], t_a[:, :]))
                V.scalar_tensor_tensor(shift[:, :], mean[:, :], -1.0, rstd[:, :], ALU.mult, ALU.mult).then_inc(norm_ready, 1)
                dve.sem_inc(proj_read, 2)
                dve.sem_inc(rows_stored[0], 32)
                dve.sem_inc(rows_stored[1], 32)

                def body(T, i, b, last):
                    dve.wait_ge(proj_done, T * 2 + 1)
                    dve.wait_ge(rows_stored[b], i * 32 + 32)
                    V.tensor_tensor(qv_out[:, b, :], bank[2 + 2 * b][:, :], bias[:, 0:2 * D], ALU.add).then_inc(rows_ready, 1)
                    dve.wait_ge(proj_done, T * 2 + 2)
                    V.tensor_tensor(ks[:, bass.ds(T, 1), :, :].rearrange("p o k d -> p (o k d)"), bank[3 + 2 * b][:, :],
                                    bias[:, 2 * D:4 * D], ALU.add).then_inc(proj_read, 1)
                pairs(dve, body)

            @block.scalar
            def _(act):
                act.wait_ge(var_ready, 1)
                A.sqrt(t_a[:, :], t_b[:, :]).then_inc(root_ready, 1)
                act.wait_ge(norm_ready, 1)

                def normalise(T, b):
                    A.activation(h_buf[:, b, :], xs[:, bass.ds(T, 1), :].rearrange("p o d -> p (o d)"), ACT.Relu,
                                 bias=shift[:, bass.ds(T, 1)], scale=rstd[:, bass.ds(T, 1)]).then_inc(h_ready, 1)
                act.sem_inc(hT_ready, 1)
                act.sem_inc(h_turned, 1)
                normalise(0, 0)

                def body(T, i, b, last):
                    if not last:
                        act.wait_ge(h_turned, T + 1)
                        normalise(T + 1, 1 - b)
                    act.wait_ge(h_turned, T + 2)
                    A.copy(hT[:, b, :, :].rearrange("p c n -> p (c n)"), bank[b][:, 0:2 * P]).then_inc(hT_ready, 1)
                pairs(act, body)

            @block.tensor
            def _(pe):
                def turn_h(b):
                    for c in range(2):
                        last = T_.transpose(bank[b][:, c * P:(c + 1) * P], h_buf[:, b, c * P:(c + 1) * P], ident[:, :])
                    last.then_inc(h_turned, 1)
                pe.wait_ge(h_ready, 1)
                turn_h(0)

                def body(T, i, b, last):
                    if not last:
                        pe.wait_ge(h_ready, T + 2)
                        pe.wait_ge(hT_ready, T + 1)
                        turn_h(1 - b)
                    pe.wait_ge(hT_ready, T + 2)
                    pe.wait_ge(proj_read, T + 1)
                    for half in range(2):
                        for c in range(2):
                            mm = T_.matmul(bank[2 + 2 * b + half][:, :], hT[:, b, c, :], wT[:, c, half * 512:(half + 1) * 512],
                                           start=(c == 0), stop=(c == 1))
                        mm.then_inc(proj_done, 1)
                pairs(pe, body)

            @block.sync
            def _(sp):
                def body(T, i, b, last):
                    sp.wait_ge(rows_ready, T + 1)
                    sp.dma_start(q_tab[bass.ds(T * P, P), :], qv_out[:, b, 0:D]).then_inc(rows_stored[b], 16)
                    sp.dma_start(v_tab[bass.ds(T * P, P), :], qv_out[:, b, D:2 * D]).then_inc(rows_stored[b], 16)
                pairs(sp, body)
                sp.wait_ge(rows_stored[0], 32 * (NT // 2 + 1) + 32)
                sp.wait_ge(rows_stored[1], 32 * (NT // 2) + 32)

        def gather_rows(tag, table, slots_used, group):
            got = [sem(f"{tag}_got{u}") for u in range(U)]
            index_ready, claimed = sem(f"{tag}_index_ready"), sem(f"{tag}_claimed")
            H = U // 2

            def pool_part(pool):
                with pool.Fori(0, ITERS) as i:
                    for u in range(U):
                        if u % H == 0:
                            pool.wait_ge(index_ready, i * 2 + (1 + u // H))
                            pool.sem_inc(claimed, 1)
                        if u % group == 0:
                            pool.wait_ge(slots_used, i * (U // group) + (u // group + 1))
                            pool.sem_inc(claimed, 1)
                        pool.indirect_dma_start(ring[:, u, 0:D], None, table,
                                                bass.IndirectOffsetOnAxis(ap=src_stage[:, u:u + 1], axis=0)).then_inc(got[u], 16)

            def index_first(act):
                A.copy(src_stage[:, 0:H], v_src[:, 0:H]).then_inc(index_ready, 1)
                A.copy(src_stage[:, H:U], v_src[:, H:U]).then_inc(index_ready, 1)

            def index_next(act, i):
                for half in range(2):
                    for u in range(H):
                        act.wait_ge(got[half * H + u], i * 16 + 16)
                    A.copy(src_stage[:, half * H:(half + 1) * H], v_src[:, bass.ds(i * U + (U + half * H), H)]).then_inc(index_ready, 1)
            return got, pool_part, index_first, index_next

        def load_node_tiles(eng, i):
            _, vals = nc.values_load_multi_w_load_instructions(t_int[0:1, bass.ds(i * U, U)], engines=[eng.engine],
                                                               min_val=0, max_val=NT - 1, skip_runtime_bounds_check_because='T(t) is clamped by its construction')
            return vals

        stage.close()
        loc_bc = tb("loc_bc", [P, 1, U * P], BF16)
        hotT = tb("hotT", [P, U, P])
        prod = tb("prod", [P, U, D])
        with nc.Block() as block:
            loc_in = sem("loc_in")
            hotT_ready, k_spread, qk_used = sem("hotT_ready"), sem("k_spread"), sem("qk_used")
            got, pool_part, index_first, index_next = gather_rows("q", q_tab, qk_used, 2)

            @block.gpsimd
            def _(pool):
                pool_part(pool)

            @block.scalar
            def _(act):
                index_first(act)
                with act.Fori(0, ITERS) as i:
                    index_next(act, i)

            @block.sync
            def _(sp):
                with sp.Fori(0, ITERS) as i:
                    sp.wait_ge(hotT_ready, i + 1)
                    sp.dma_start(loc_bc[:, 0, :], local_tab[bass.ds(i * U, U), :].rearrange("t e -> (t e)").partition_broadcast(P)).then_inc(loc_in, 16)
                sp.wait_ge(loc_in, 16 * ITERS)

            @block.tensor
            def _(pe):
                with pe.Fori(0, ITERS) as i:
                    tiles = load_node_tiles(pe, i)
                    pe.wait_ge(hotT_ready, i + 2)
                    for j in range(U // 2):
                        pe.wait_ge(qk_used, i * (U // 2) + (j + 1))
                        for u in (2 * j, 2 * j + 1):
                            mm = T_.matmul(bank[j][:, (u % 2) * D:(u % 2 + 1) * D], hotT[:, u, :],
                                           ks[:, bass.ds(tiles[u], 1), 0, :], start=True, stop=True)
                        mm.then_inc(k_spread, 1)

            @block.vector
            def _(dve):
                dve.sem_inc(hotT_ready, 1)
                dve.sem_inc(qk_used, U // 2)
                with dve.Fori(0, ITERS) as i:
                    dve.wait_ge(loc_in, i * 16 + 16)
                    V.tensor_scalar(hotT[:, :, :].rearrange("p u e -> p (u e)"), loc_bc[:, 0, :], pcol[:, 0:1], None,
                                    ALU.is_equal).then_inc(hotT_ready, 1)
                    for j in range(U // 2):
                        dve.wait_ge(k_spread, i * (U // 2) + (j + 1))
                        dve.wait_ge(got[2 * j], i * 16 + 16)
                        dve.wait_ge(got[2 * j + 1], i * 16 + 16)
                        V.tensor_tensor(prod[:, 2 * j:2 * j + 2, :], ring[:, 2 * j:2 * j + 2, 0:D],
                                        bank[j][:, :].rearrange("p (u d) -> p u d", u=2), ALU.mult).then_inc(qk_used, 1)
                    dve.wait_ge(qk_used, i * (U // 2) + U)
                    V.tensor_reduce(score[:, bass.ds(i * (U * HEADS), U * HEADS)],
                                    prod[:, :, :].rearrange("p u (h d) -> p (u h) d", h=HEADS), AX.X, ALU.add)

        stage.close()
        seg = tb("seg", [SR, SC, HEADS, P])
        seg2 = tb("seg2", [SR, SC, HEADS, P])
        cuts = tb("cuts", [SR, SC, HEADS, P])
        reach = tb("reach", [SR, SC, P])
        cut_all = tb("cut_all", [SR, SC])
        ends = tb("ends", [SR, SC, 2, HEADS])
        firsts = tb("firsts", [SR, SC, HEADS])
        head_ends = tb("head_ends", [HEADS, STEPS])
        head_cuts = tb("head_cuts", [HEADS, STEPS])
        head_first = tb("head_first", [HEADS, STEPS])
        back_cuts = tb("back_cuts", [HEADS, STEPS])
        carry = tb("carry", [HEADS, STEPS + 1])
        carry_in = tb("carry_in", [HEADS, STEPS])
        carry_col = tb("carry_col", [SR, SC, HEADS])

        with nc.Block() as block:
            masked, rows_turned, rows_copied = sem("masked"), sem("rows_turned"), sem("rows_copied")
            ends_ready, ends_turned, carry_ready, carry_turned = sem("ends_ready"), sem("ends_turned"), sem("carry_ready"), sem("carry_turned")
            max_ready, max_turned, shifted = sem("max_ready"), sem("max_turned"), sem("shifted")
            by_step = score[:, :].rearrange("p (t h) -> p t h", h=HEADS)

            @block.tensor
            def _(pe):
                pe.wait_ge(masked, 1)
                for sc in range(SC):
                    for h in range(HEADS):
                        last = T_.transpose(bank[sc][0:SR, h * P:(h + 1) * P], by_step[:, sc * SR:(sc + 1) * SR, h], ident[:, :])
                    last.then_inc(rows_turned, 1)
                pe.wait_ge(ends_ready, 1)
                for sc in range(SC):
                    T_.transpose(bank[7][0:HEADS, sc * SR:(sc + 1) * SR], firsts[:, sc, :], ident[0:SR, 0:SR])
                for way in range(2):
                    pe.wait_ge(ends_ready, way + 1)
                    for sc in range(SC):
                        T_.transpose(bank[4][0:HEADS, sc * SR:(sc + 1) * SR], ends[:, sc, 0, :], ident[0:SR, 0:SR])
                        last = T_.transpose(bank[5][0:HEADS, sc * SR:(sc + 1) * SR], ends[:, sc, 1, :], ident[0:SR, 0:SR])
                    last.then_inc(ends_turned, 1)
                    pe.wait_ge(carry_ready, way + 1)
                    for sc in range(SC):
                        last = T_.transpose(bank[6][0:SR, sc * HEADS:(sc + 1) * HEADS], carry_in[:, sc * SR:(sc + 1) * SR],
                                            ident[0:HEADS, 0:HEADS])
                    last.then_inc(carry_turned, 1)
                for h in range(HEADS):
                    for sc in range(SC):
                        if h == 0:
                            pe.wait_ge(max_ready, sc + 1)
                        last = T_.transpose(bank[h][:, sc * SR:(sc + 1) * SR], seg[:, sc, h, :], ident[0:SR, 0:SR])
                    last.then_inc(max_turned, 1)

            @block.scalar
            def _(act):
                for sc in range(SC):
                    act.wait_ge(rows_turned, sc + 1)
                    A.copy(seg[:, sc, :, :].rearrange("p h e -> p (h e)"), bank[sc][0:SR, :]).then_inc(rows_copied, 1)
                act.wait_ge(shifted, HEADS)
                A.activation(score[:, :], score[:, :], ACT.Exp, scale=SCALE)

            @block.vector
            def _(dve):
                chain = Chain(dve, "max_chain")
                f = chain.follow

                def rows(t, sc):
                    return t[:, sc, :, :].rearrange("p h e -> p (h e)")

                V.tensor_tensor(by_step, by_step, maskb[:, :].unsqueeze(2).to_broadcast([P, STEPS, HEADS]), ALU.add).then_inc(masked, 1)
                f(V.tensor_copy(cuts[:, :, :, :], row_start[:, :, :].unsqueeze(2).to_broadcast([SR, SC, HEADS, P])))
                f(V.memset(cuts[:, :, :, 0], NEG))
                for sc in range(SC):
                    dve.wait_ge(rows_copied, sc + 1)
                    V.tensor_tensor_scan(rows(seg2, sc), rows(cuts, sc), rows(seg, sc), NEG, ALU.add, ALU.max)
                for sc in range(SC):
                    V.tensor_tensor_scan(reach[:, sc, :], row_start[:, sc, :], row_start[:, sc, :], 0.0, ALU.min, ALU.min)
                f(V.tensor_reduce(cut_all[:, :], row_start[:, :, :], AX.X, ALU.min))
                V.tensor_copy(firsts[:, :, :], row_start[:, :, 0].unsqueeze(2).to_broadcast([SR, SC, HEADS]))
                V.tensor_copy(ends[:, :, 0, :], seg2[:, :, :, P - 1])
                V.tensor_copy(ends[:, :, 1, :], cut_all[:, :].unsqueeze(2).to_broadcast([SR, SC, HEADS])).then_inc(ends_ready, 1)
                dve.wait_ge(ends_turned, 1)
                V.tensor_copy(head_ends[:, :], bank[4][0:HEADS, 0:STEPS])
                V.tensor_copy(head_cuts[:, :], bank[5][0:HEADS, 0:STEPS])
                V.tensor_copy(head_first[:, :], bank[7][0:HEADS, 0:STEPS])
                f(V.memset(carry[:, :], NEG))
                f(V.tensor_tensor_scan(carry[:, 1:STEPS + 1], head_cuts[:, :], head_ends[:, :], NEG, ALU.add, ALU.max))
                V.tensor_copy(carry_in[:, :], carry[:, 0:STEPS]).then_inc(carry_ready, 1)
                dve.wait_ge(carry_turned, 1)
                f(V.tensor_copy(carry_col[:, :, :], bank[6][0:SR, 0:SC * HEADS].rearrange("p (c h) -> p c h", c=SC)))
                for sc in range(SC):
                    for h in range(HEADS):
                        last = V.scalar_tensor_tensor(seg2[:, sc, h, :], reach[:, sc, :], carry_col[:, sc, h:h + 1], seg2[:, sc, h, :], ALU.add, ALU.max)
                f(last)
                V.memset(cuts[:, :, :, P - 1], NEG)
                f(V.tensor_copy(cuts[:, :, :, 0:P - 1], row_start[:, :, 1:P].unsqueeze(2).to_broadcast([SR, SC, HEADS, P - 1])))
                for sc in range(SC):
                    last = V.tensor_tensor_scan(rows(seg, sc)[:, ::-1], rows(cuts, sc)[:, ::-1], rows(seg2, sc)[:, ::-1], NEG, ALU.add, ALU.max)
                f(last)
                f(V.memset(cuts[:, :, 0, P - 1], 0.0))
                for sc in range(SC):
                    V.tensor_tensor_scan(reach[:, sc, ::-1], cuts[:, sc, 0, ::-1], cuts[:, sc, 0, ::-1], 0.0, ALU.min, ALU.min)
                f(V.tensor_copy(ends[:, :, 0, :], seg[:, :, :, 0]))
                V.tensor_copy(ends[:, :, 1, :], reach[:, :, 0].unsqueeze(2).to_broadcast([SR, SC, HEADS])).then_inc(ends_ready, 1)
                dve.wait_ge(ends_turned, 2)
                V.tensor_copy(head_ends[:, :], bank[4][0:HEADS, 0:STEPS])
                V.tensor_copy(head_cuts[:, :], bank[5][0:HEADS, 0:STEPS])
                f(V.memset(carry_in[:, :], NEG))
                f(V.tensor_tensor(back_cuts[:, 0:STEPS - 1], head_cuts[:, 0:STEPS - 1], head_first[:, 1:STEPS], ALU.add))
                f(V.memset(back_cuts[:, STEPS - 1:STEPS], NEG))
                f(V.tensor_tensor_scan(carry[:, 0:STEPS][:, ::-1], back_cuts[:, ::-1], head_ends[:, ::-1], NEG, ALU.add, ALU.max))
                V.tensor_tensor(carry_in[:, 0:STEPS - 1], carry[:, 1:STEPS], head_first[:, 1:STEPS], ALU.add).then_inc(carry_ready, 1)
                dve.wait_ge(carry_turned, 2)
                f(V.tensor_copy(carry_col[:, :, :], bank[6][0:SR, 0:SC * HEADS].rearrange("p (c h) -> p c h", c=SC)))
                for sc in range(SC):
                    for h in range(HEADS):
                        last = V.scalar_tensor_tensor(seg[:, sc, h, :], reach[:, sc, :], carry_col[:, sc, h:h + 1], seg[:, sc, h, :], ALU.add, ALU.max)
                    last.then_inc(max_ready, 1)
                for h in range(HEADS):
                    dve.wait_ge(max_turned, h + 1)
                    V.tensor_tensor(by_step[:, :, h], by_step[:, :, h], bank[h][:, 0:STEPS], ALU.subtract).then_inc(shifted, 1)

        stage.close()
        hot = tb("hot", [P, U, P])
        with nc.Block() as block:
            sums_done, sums_added, msg_ready, ex_ready = sem("sums_done"), sem("sums_added"), sem("msg_ready"), sem("ex_ready")
            got, pool_part, index_first, index_next = gather_rows("v", v_tab, sums_done, 1)

            @block.gpsimd
            def _(pool):
                pool_part(pool)

            @block.scalar
            def _(act):
                index_first(act)
                with act.Fori(0, ITERS) as i:
                    act.wait_ge(sums_done, i * U + U)
                    A.copy(ring[:, :, DEN:DEN + HEADS], score[:, bass.ds(i * (U * HEADS), U * HEADS)].rearrange("p (u h) -> p u h", u=U)).then_inc(ex_ready, 1)
                    index_next(act, i)

            @block.tensor
            def _(pe):
                pe.sem_inc(sums_done, U)
                with pe.Fori(0, ITERS) as i:
                    pe.wait_ge(ex_ready, i + 1)
                    for u in range(U):
                        if u % 2 == 0:
                            pe.wait_ge(msg_ready, i * (U // 2) + (u // 2 + 1))
                        pe.wait_ge(sums_added, i * U + (u + 1))
                        T_.matmul(bank[u][:, 0:DEG + 1], hot[:, u, :], ring[:, u, 0:DEG + 1], start=True, stop=True).then_inc(sums_done, 1)

            @block.vector
            def _(dve):
                dve.sem_inc(sums_added, U)
                with dve.Fori(0, ITERS) as i:
                    tiles = load_node_tiles(dve, i)

                    def add(u):
                        dve.wait_ge(sums_done, i * U + (U + u + 1))
                        a = acc[:, bass.ds(tiles[u], 1), 0:DEG + 1].rearrange("p o d -> p (o d)")
                        V.tensor_tensor(a, a, bank[u][:, 0:DEG + 1], ALU.add).then_inc(sums_added, 1)
                        if u < U - 1:
                            dve.wait_ge(sums_added, i * U + (U + u + 1))
                    dve.wait_ge(sums_added, i * U + U)
                    V.tensor_tensor(hot[:, :, :], iota_f[:, 0:P].unsqueeze(1).to_broadcast([P, U, P]),
                                    v_loc[:, bass.ds(i * U, U)].unsqueeze(2).to_broadcast([P, U, P]), ALU.is_equal)
                    for j in range(U // 2):
                        dve.wait_ge(got[2 * j], i * 16 + 16)
                        dve.wait_ge(got[2 * j + 1], i * 16 + 16)
                        rows_ = ring[:, 2 * j:2 * j + 2, 0:D].rearrange("p u (h d) -> p u h d", h=HEADS)
                        V.tensor_tensor(rows_, rows_, score[:, bass.ds(i * (U * HEADS) + 2 * j * HEADS, 2 * HEADS)]
                                        .rearrange("p (u h) -> p u h", u=2).unsqueeze(3).to_broadcast([P, 2, HEADS, DH]), ALU.mult).then_inc(msg_ready, 1)
                        if j > 0:
                            add(2 * j - 2)
                            add(2 * j - 1)
                    add(U - 2)
                    add(U - 1)

        stage.close()
        sA = tb("sA", [P, NB, D])
        sB = tb("sB", [P, NB, D])
        sC = tb("sC", [P, NB, D])
        with nc.Block() as block:
            z_ready, e_ready, var_ready, root_ready, relu_ready, relu_used, neg_used = [sem("mid_" + n) for n in "z e var root relu relu_used neg_used".split()]
            norm2_ready, h2_ready, h2_stored = sem("norm2_ready"), sem("h2_ready"), sem("h2_stored")
            normed, normed_used = sem("normed"), sem("normed_used")

            def grp(t, g, lo=0, n=D):
                return t[:, bass.ds(g * NB, NB), lo:lo + n]

            @block.vector
            def _(dve):
                chain = Chain(dve, "between_chain")
                f = chain.follow
                f(V.tensor_scalar(rden[:, :, :], acc[:, :, DEN:DEN + HEADS], 1e-30, None, ALU.max))
                V.reciprocal(rden[:, :, :], rden[:, :, :])
                f(V.tensor_scalar(rdeg[:, :], acc[:, :, DEG], 1.0, None, ALU.max))
                f(V.reciprocal(rdeg[:, :], rdeg[:, :]))
                with dve.Fori(0, NG) as g:
                    chain.enter(g, 5)
                    mean_v = grp(acc, g)
                    f(V.tensor_tensor(mean_v.rearrange("p t (h d) -> p t h d", h=HEADS), mean_v.rearrange("p t (h d) -> p t h d", h=HEADS),
                                      rden[:, bass.ds(g * NB, NB), :].unsqueeze(3).to_broadcast([P, NB, HEADS, DH]), ALU.mult))
                    skip_v = ks[:, bass.ds(g * NB, NB), 1, :]
                    f(V.tensor_tensor(skip_v, skip_v, mean_v, ALU.subtract))
                    V.tensor_tensor(sA[:, :, :], skip_v, gate_u[:, :].unsqueeze(1).to_broadcast([P, NB, D]), ALU.mult)
                    f(V.tensor_tensor(sB[:, :, :], mean_v, gate_w[:, :].unsqueeze(1).to_broadcast([P, NB, D]), ALU.mult))
                    f(V.tensor_tensor(sA[:, :, :], sA[:, :, :], sB[:, :, :], ALU.add))
                    f(V.tensor_reduce(zz[:, bass.ds(g * NB, NB)], sA[:, :, :], AX.X, ALU.add))
                chain.leave(NG)
                V.tensor_scalar(zz[:, :], zz[:, :], bg[:, 0:1], None, ALU.add).then_inc(z_ready, 1)
                dve.wait_ge(e_ready, 1)
                f(V.tensor_scalar(zz[:, :], zz[:, :], 1.0, None, ALU.add))
                f(V.reciprocal(zz[:, :], zz[:, :]))
                with dve.Fori(0, NG) as g:
                    chain.enter(g, 3)
                    f(V.tensor_tensor(sA[:, :, :], ks[:, bass.ds(g * NB, NB), 1, :], zz[:, bass.ds(g * NB, NB)].unsqueeze(2).to_broadcast([P, NB, D]), ALU.mult))
                    f(V.tensor_tensor(grp(acc, g), grp(acc, g), sA[:, :, :], ALU.add))
                    chain.pass_wait()
                    for n in range(NB):
                        last = V.bn_stats(stats[:, bass.ds(g * NB + n, 1), :], acc[:, bass.ds(g * NB + n, 1), 0:D])
                    f(last)
                chain.leave(NG)
                moments(f)
                V.tensor_copy(sA[:, 0, 0:1], sA[:, 0, 0:1]).then_inc(var_ready, 1)
                dve.wait_ge(root_ready, 1)
                f(V.reciprocal(rstd[:, :], t_a[:, :]))
                V.scalar_tensor_tensor(shift[:, :], mean[:, :], -1.0, rstd[:, :], ALU.mult, ALU.mult).then_inc(norm2_ready, 1)
                with dve.Fori(0, NG) as g:
                    chain.enter(g, 6)
                    dve.wait_ge(normed, g * NB + NB)
                    f(V.tensor_tensor(sA[:, :, :], grp(acc, g), lnw[:, :].unsqueeze(1).to_broadcast([P, NB, D]), ALU.mult))
                    f(V.tensor_tensor(sA[:, :, :], sA[:, :, :], lnb[:, :].unsqueeze(1).to_broadcast([P, NB, D]), ALU.add))
                    V.tensor_scalar(sB[:, :, :], sA[:, :, :], 0.0, pa[:, 0:1], ALU.min, ALU.mult)
                    f(V.tensor_scalar(sC[:, :, :], sA[:, :, :], 0.0, None, ALU.max))
                    f(V.tensor_tensor(sB[:, :, :], sB[:, :, :], sC[:, :, :], ALU.add))
                    f(V.tensor_tensor(grp(xs, g), grp(xs, g), sB[:, :, :], ALU.add))
                    chain.pass_wait()
                    for n in range(NB):
                        last = V.bn_stats(stats[:, bass.ds(g * NB + n, 1), :], xs[:, bass.ds(g * NB + n, 1), :])
                    f(last)
                chain.leave(NG)
                moments(f)
                V.tensor_copy(sA[:, 0, 0:1], sA[:, 0, 0:1]).then_inc(var_ready, 1)
                dve.wait_ge(root_ready, 2)
                f(V.reciprocal(rstd[:, :], t_a[:, :]))
                V.scalar_tensor_tensor(shift[:, :], mean[:, :], -1.0, rstd[:, :], ALU.mult, ALU.mult).then_inc(norm2_ready, 1)

            @block.scalar
            def _(act):
                act.wait_ge(z_ready, 1)
                A.activation(zz[:, :], zz[:, :], ACT.Exp, scale=-1.0).then_inc(e_ready, 1)
                act.wait_ge(var_ready, 1)
                A.sqrt(t_a[:, :], t_b[:, :]).then_inc(root_ready, 1)
                act.wait_ge(norm2_ready, 1)
                with act.Fori(0, NT) as T:
                    row = acc[:, bass.ds(T, 1), 0:D].rearrange("p o d -> p (o d)")
                    A.activation(row, row, ACT.Identity, bias=shift[:, bass.ds(T, 1)], scale=rstd[:, bass.ds(T, 1)]).then_inc(normed, 1)
                act.wait_ge(var_ready, 2)
                A.sqrt(t_a[:, :], t_b[:, :]).then_inc(root_ready, 1)
                act.wait_ge(norm2_ready, 2)
                with act.Fori(0, NT) as T:
                    A.activation(ks[:, bass.ds(T, 1), 1, :].rearrange("p o d -> p (o d)"), xs[:, bass.ds(T, 1), :].rearrange("p o d -> p (o d)"), ACT.Relu,
                                 bias=shift[:, bass.ds(T, 1)], scale=rstd[:, bass.ds(T, 1)]).then_inc(h2_ready, 1)

            @block.sync
            def _(sp):
                with sp.Fori(0, NG) as g:
                    sp.wait_ge(h2_ready, g * NB + NB)
                    sp.dma_start(h_tab[bass.ds(g * (NB * P), NB * P), :].rearrange("(t p) d -> p t d", p=P), ks[:, bass.ds(g * NB, NB), 1, :]).then_inc(h2_stored, 16)
                sp.wait_ge(h2_stored, 16 * NG)

            @block.gpsimd
            def _(pool):
                pool.wait_ge(normed, NT)
                pool.wait_ge(var_ready, 2)

        with nc.Block() as block:
            @block.gpsimd
            def _(pool):
                G.memset(acc[:, :, 0:D], 0.0)

        stage.close()
        hot = tb("hot2", [P, U, P])
        with nc.Block() as block:
            sums_done, sums_added, hot_ready = sem("n_sums_done"), sem("n_sums_added"), sem("n_hot_ready")
            got, pool_part, index_first, index_next = gather_rows("h", h_tab, sums_done, 1)

            @block.gpsimd
            def _(pool):
                pool_part(pool)

            @block.scalar
            def _(act):
                index_first(act)
                with act.Fori(0, ITERS) as i:
                    index_next(act, i)

            @block.tensor
            def _(pe):
                pe.sem_inc(sums_done, U)
                with pe.Fori(0, ITERS) as i:
                    for u in range(U):
                        pe.wait_ge(hot_ready, i * U + (u + 1))
                        pe.wait_ge(got[u], i * 16 + 16)
                        pe.wait_ge(sums_added, i * U + (u + 1))
                        T_.matmul(bank[u][:, 0:D], hot[:, u, :], ring[:, u, 0:D], start=True, stop=True).then_inc(sums_done, 1)

            @block.vector
            def _(dve):
                dve.sem_inc(sums_added, U)
                with dve.Fori(0, ITERS) as i:
                    tiles = load_node_tiles(dve, i)
                    for u in range(U):
                        dve.wait_ge(sums_added, i * U + U)
                        V.tensor_scalar(hot[:, u, :], iota_f[:, 0:P], v_loc[:, bass.ds(i * U + u, 1)], v_wgt[:, bass.ds(i * U + u, 1)],
                                        ALU.is_equal, ALU.mult).then_inc(hot_ready, 1)
                    for u in range(U):
                        dve.wait_ge(sums_done, i * U + (U + u + 1))
                        if u > 0:
                            dve.wait_ge(sums_added, i * U + (U + u))
                        a = acc[:, bass.ds(tiles[u], 1), 0:D].rearrange("p o d -> p (o d)")
                        V.tensor_tensor(a, a, bank[u][:, 0:D], ALU.add).then_inc(sums_added, 1)

        stage.close()
        h_buf = tb("mean_buf", [P, 2, D])
        hT = tb("in_T", [P, 2, 4, P])
        res = tb("res", [P, 2, D])
        with nc.Block() as block:
            mean_ready, turned, inT_ready, out_done, out_ready = [sem("f_" + n) for n in "mean turned inT out_done out_ready".split()]
            stored = [sem("f_stored0"), sem("f_stored1")]

            @block.scalar
            def _(act):
                def mean_of(T, b):
                    A.activation(h_buf[:, b, :], acc[:, bass.ds(T, 1), 0:D].rearrange("p o d -> p (o d)"), ACT.Copy,
                                 scale=rdeg[:, bass.ds(T, 1)]).then_inc(mean_ready, 1)
                    A.copy(res[:, b, :], ks[:, bass.ds(T, 1), 1, :].rearrange("p o d -> p (o d)")).then_inc(mean_ready, 1)
                act.sem_inc(inT_ready, 1)
                act.sem_inc(turned, 1)
                mean_of(0, 0)

                def body(T, i, b, last):
                    if not last:
                        act.wait_ge(turned, T + 1)
                        mean_of(T + 1, 1 - b)
                    act.wait_ge(turned, T + 2)
                    A.copy(hT[:, b, :, :].rearrange("p c n -> p (c n)"), bank[b][:, :]).then_inc(inT_ready, 1)
                pairs(act, body)

            @block.tensor
            def _(pe):
                def turn(T, b):
                    for c in range(4):
                        t = h_buf if c < 2 else res
                        last = T_.transpose(bank[b][:, c * P:(c + 1) * P], t[:, b, (c % 2) * P:(c % 2 + 1) * P], ident[:, :])
                    last.then_inc(turned, 1)
                pe.wait_ge(mean_ready, 2)
                turn(0, 0)

                def body(T, i, b, last):
                    if not last:
                        pe.wait_ge(mean_ready, T * 2 + 4)
                        pe.wait_ge(inT_ready, T + 1)
                        turn(T + 1, 1 - b)
                    pe.wait_ge(inT_ready, T + 2)
                    pe.wait_ge(out_ready, T + 1)
                    for c in range(4):
                        mm = T_.matmul(bank[2 + b][:, 0:D], hT[:, b, c, :], w1T[:, c, :], start=(c == 0), stop=(c == 3))
                    mm.then_inc(out_done, 1)
                pairs(pe, body)

            @block.vector
            def _(dve):
                chain = Chain(dve, "final_chain")
                f = chain.follow
                dve.sem_inc(out_ready, 2)
                f(V.tensor_tensor(xs[:, :, :], xs[:, :, :], b1s[:, :].unsqueeze(1).to_broadcast([P, NT, D]), ALU.add))

                def body(T, i, b, last):
                    dve.wait_ge(out_done, T + 1)
                    row = xs[:, bass.ds(T, 1), :].rearrange("p o d -> p (o d)")
                    V.tensor_tensor(row, row, bank[2 + b][:, 0:D], ALU.add).then_inc(out_ready, 1)
                pairs(dve, body)

            @block.sync
            def _(sp):
                with sp.Fori(0, NT - 1) as T:
                    sp.wait_ge(out_ready, T + 3)
                    sp.dma_start(out[bass.ds(T * P, P), :], xs[:, bass.ds(T, 1), :].rearrange("p o d -> p (o d)")).then_inc(stored[0], 16)
                sp.wait_ge(out_ready, NT + 2)
                sp.dma_start(out[(NT - 1) * P:N, :], xs[0:LAST_ROWS, NT - 1, :]).then_inc(stored[1], 16)
                sp.wait_ge(stored[0], 16 * (NT - 1))
                sp.wait_ge(stored[1], 16)
        stage.close()


_INS = ['x', 'src', 'dst', 'edge_weight1', 'L0_gnn_Wq', 'L0_gnn_bq', 'L0_gnn_Wk', 'L0_gnn_bk', 'L0_gnn_Wv', 'L0_gnn_bv',
        'L0_gnn_Wskip', 'L0_gnn_bskip', 'L0_gnn_Wgate', 'L0_gnn_bgate', 'L0_gnn_ln_w', 'L0_gnn_ln_b',
        'L0_gnn_prelu_a', 'L1_gnn_W', 'L1_gnn_b']
_OUTS = [((3125, 256), 'float32')]


def kernel(**inputs):
    import numpy as _np
    import concourse.bacc as _bacc
    from concourse import mybir as _mybir
    from concourse.bass_utils import run_bass_kernel_spmd as _run

    nc = _bacc.Bacc("TRN2", target_bir_lowering=False, num_devices=1)
    arrays, args = {}, []
    for name in _INS:
        a = _np.ascontiguousarray(inputs[name])
        if a.ndim == 0:
            a = a.reshape(1)
        arrays[f"in_{name}_dram"] = a
        args.append(nc.dram_tensor(f"in_{name}_dram", a.shape, _mybir.dt.from_np(a.dtype), kind="ExternalInput").ap())
    for i, (shape, dtype) in enumerate(_OUTS):
        dt = _mybir.dt.from_np(_np.dtype(dtype))
        args.append(nc.dram_tensor(f"out_{i}_dram", shape, dt, kind="ExternalOutput").ap())
    gnn_kernel(nc, *args)
    r = _run(nc, [arrays], core_ids=[0])
    got = tuple(r.results[0][f"out_{i}_dram"] for i in range(len(_OUTS)))
    return got[0]
```

```python
import concourse.bass as bass
from concourse import mybir
from contextlib import ExitStack

F32 = mybir.dt.float32
BF16 = mybir.dt.bfloat16
I32 = mybir.dt.int32
ALU = mybir.AluOpType
ACT = mybir.ActivationFunctionType
AX = mybir.AxisListType

P = 128
HEADS = 4


def gnn_kernel(nc, x, src, dst, edge_weight, Wq, bq, Wk, bk, Wv, bv, Wskip, bskip, Wgate, bgate,
               ln_w, ln_b, prelu_a, W1, b1, out):
    N, D = x.shape
    E = src.shape[0]
    DH = D // HEADS
    NT = -(-N // P)
    LAST_ROWS = N - (NT - 1) * P
    ET = -(-E // P)
    LAST_EDGES = E - (ET - 1) * P
    STEPS = ET + NT - 1
    U = 20
    ITERS = STEPS // U
    assert STEPS % U == 0
    EC = 4
    ER = ET // EC
    SC = 4
    SR = STEPS // SC
    assert ET % EC == 0 and STEPS % SC == 0 and ER <= P and SR <= P
    LAST_C = (ET - 1) // ER
    LAST_P = (ET - 1) % ER
    NB = 5
    NG = NT // NB
    assert NT % NB == 0
    SCALE = float(DH) ** -0.5
    NEG = -1.0e30
    FAR = 1 << 20
    DEN = D
    DEG = D + HEADS
    AW = D + 8

    qv_tab = nc.dram_tensor("qv_tab", (NT * P, 2 * D), F32, kind="Internal").ap()
    v_rows = nc.dram_tensor("v_rows", (STEPS, P, D), F32, kind="Internal").ap()
    h_tab = nc.dram_tensor("h_tab", (NT * P, D), F32, kind="Internal").ap()
    local_tab = nc.dram_tensor("local_tab", (STEPS + U, P), BF16, kind="Internal").ap()

    with ExitStack() as ctx:
        def sb(name, shape, dt=F32):
            return ctx.enter_context(nc.sbuf_tensor(name, shape, dt))

        stage = ExitStack()

        def tb(name, shape, dt=F32):
            return stage.enter_context(nc.sbuf_tensor(name, shape, dt))

        def sem(name):
            return ctx.enter_context(nc.semaphore(name))

        xs = sb("xs", [P, NT, D])
        ks = sb("ks", [P, NT, 2, D])
        w1T = sb("w1T", [P, 4, D])
        gate = sb("gate", [P, 3 * D])
        gate_u = sb("gate_u", [P, D])
        gate_w = sb("gate_w", [P, D])
        lnw = sb("lnw", [P, D])
        lnb = sb("lnb", [P, D])
        b1s = sb("b1s", [P, D])
        bg = sb("bg", [P, 1])
        pa = sb("pa", [P, 1])
        ident = sb("ident", [P, P])
        ones = sb("ones", [P, P])
        iota_f = sb("iota_f", [P, STEPS])
        t_row = sb("t_row", [P, STEPS])
        t_int = sb("t_int", [1, STEPS], I32)
        v_src = sb("v_src", [P, STEPS + U], I32)
        v_loc = sb("v_loc", [P, STEPS + U])
        v_wgt = sb("v_wgt", [P, STEPS])
        maskb = sb("maskb", [P, STEPS])
        row_start = sb("row_start", [SR, SC, P])
        src_stage = sb("src_stage", [P, U], I32)
        stats = sb("stats", [P, NT, 6])
        mean = sb("mean", [P, NT])
        rstd = sb("rstd", [P, NT])
        shift = sb("shift", [P, NT])
        t_a = sb("t_a", [P, NT])
        t_b = sb("t_b", [P, NT])
        pcol = sb("pcol", [P, 1])
        score = sb("score", [P, STEPS * HEADS])
        zz = sb("zz", [P, NT])
        rden = sb("rden", [P, NT, HEADS])
        rdeg = sb("rdeg", [P, NT])

        passed, passed2 = sem("passed"), sem("passed2")

        bank = [ctx.enter_context(nc.psum_tensor(f"bank{i}", [P, 512], F32)) for i in range(8)]

        class Chain:

            def __init__(self, eng, name):
                self.eng, self.sem, self.n = eng, sem(name), 0

            def follow(self, ins):
                ins.then_inc(self.sem, 1)
                self.n = self.n + 1
                self.eng.wait_ge(self.sem, self.n)

            def pass_wait(self):
                self.eng.sem_inc(passed, 1)

            def enter(self, i, per):
                self.base, self.per = self.n, per
                self.n = i * per + self.base

            def leave(self, count):
                self.n = self.base + self.per * count

        V, A, G, T_ = nc.vector, nc.scalar, nc.gpsimd, nc.tensor

        proj = ExitStack()

        def pj(name, shape, dt=F32):
            return proj.enter_context(nc.sbuf_tensor(name, shape, dt))

        wT = pj("wT", [P, 2, 4 * D])
        bias = pj("bias", [P, 4 * D])

        wnat = tb("wnat", [P, 8, D])
        w1nat = tb("w1nat", [P, 2, 2 * D])
        iota_i = tb("iota_i", [P, STEPS], I32)
        part_i = tb("part_i", [P, EC], I32)
        part_f = tb("part_f", [P, EC])
        step_i = tb("step_i", [P, SC], I32)
        step_f = tb("step_f", [P, SC])
        bound_i = tb("bound_i", [P, NT - 1], I32)
        bound_f = tb("bound_f", [P, NT - 1])
        nt_i = tb("nt_i", [P, NT - 1], I32)
        nt_f = tb("nt_f", [P, NT - 1])
        e_int = tb("e_int", [ER, 2, EC, P], I32)
        e_src = tb("e_src", [ER, EC, P])
        e_dst = tb("e_dst", [ER, EC, P])
        e_wgt = tb("e_wgt", [ER, EC, P])
        e_start = tb("e_start", [ER, EC, P])
        prev_i = tb("prev_i", [ER, EC], I32)
        prev_f = tb("prev_f", [ER, EC])
        below = tb("below", [ER, NT - 1, EC])
        turn = tb("turn", [P, NT - 1])
        reached = tb("reached", [SR, SC, NT - 1])
        tcol = tb("tcol", [SR, SC])
        tcol_bc = tb("tcol_bc", [SR, SC, P])
        r_row = tb("r_row", [P, STEPS])
        sel = tb("sel", [ER, EC, STEPS])
        row_loc = tb("row_loc", [SR, SC, P])
        row_loc_b = tb("row_loc_b", [SR, SC, P], BF16)
        row_in = tb("row_in", [SR, SC, P])
        pcol_i = tb("pcol_i", [P, 1], I32)
        with nc.Block() as block:
            x_zeroed, x_in, small_in = sem("x_zeroed"), sem("x_in"), sem("small_in")
            weights_in, edges_in, edges_padded = sem("weights_in"), sem("edges_in"), sem("edges_padded")
            consts_set, masks_set = sem("consts_set"), sem("masks_set")
            weightsT, below_ready, below_summed = sem("weightsT"), sem("below_ready"), sem("below_summed")
            tcol_ready, trow_summed = sem("tcol_ready"), sem("trow_summed")
            weights_copied = sem("weights_copied")
            sel_ready, picked, local_ready, local_out = sem("sel_ready"), sem("picked"), sem("local_ready"), sem("local_out")

            @block.sync
            def _(sp):
                sp.dma_start(wnat[:, 0:2, :], Wq.rearrange("(b p) d -> p b d", p=P)).then_inc(weights_in, 16)
                sp.dma_start(wnat[:, 2:4, :], Wv.rearrange("(b p) d -> p b d", p=P)).then_inc(weights_in, 16)
                sp.dma_start(wnat[:, 4:6, :], Wk.rearrange("(b p) d -> p b d", p=P)).then_inc(weights_in, 16)
                sp.dma_start(wnat[:, 6:8, :], Wskip.rearrange("(b p) d -> p b d", p=P)).then_inc(weights_in, 16)
                sp.dma_start(w1nat[:, :, :], W1.rearrange("(b p) d -> p b d", p=P)).then_inc(weights_in, 16)
                sp.dma_start(xs[:, 0:NT - 1, :], x[0:(NT - 1) * P, :].rearrange("(t p) d -> p t d", p=P)).then_inc(x_in, 16)
                sp.wait_ge(x_zeroed, 1)
                sp.dma_start(xs[0:LAST_ROWS, NT - 1, :], x[(NT - 1) * P:N, :]).then_inc(x_in, 16)
                for n, vec in enumerate((bq, bv, bk, bskip)):
                    sp.dma_start(bias[:, n * D:(n + 1) * D], vec.partition_broadcast(P)).then_inc(small_in, 16)
                sp.dma_start(gate[:, :], Wgate[0, :].partition_broadcast(P)).then_inc(small_in, 16)
                sp.dma_start(lnw[:, :], ln_w.partition_broadcast(P)).then_inc(small_in, 16)
                sp.dma_start(lnb[:, :], ln_b.partition_broadcast(P)).then_inc(small_in, 16)
                sp.dma_start(b1s[:, :], b1.partition_broadcast(P)).then_inc(small_in, 16)
                sp.dma_start(bg[:, :], bgate.partition_broadcast(P)).then_inc(small_in, 16)
                sp.dma_start(pa[:, :], prelu_a.partition_broadcast(P)).then_inc(small_in, 16)
                sp.wait_ge(local_ready, 1)
                sp.dma_start(local_tab[0:STEPS, :].rearrange("(c r) e -> r c e", r=SR), row_loc_b[:, :, :]).then_inc(local_out, 16)
                sp.dma_start(local_tab[STEPS:STEPS + U, :], row_loc_b[0:U, 0, :]).then_inc(local_out, 16)
                sp.wait_ge(local_out, 32)
                sp.wait_ge(small_in, 160)

            @block.gpsimd
            def _(pool):
                G.memset(e_int[:, 0, LAST_C, :], 0).then_inc(edges_padded, 1)
                G.memset(e_int[:, 1, LAST_C, :], FAR).then_inc(edges_padded, 1)
                G.memset(e_wgt[:, LAST_C, :], 0.0).then_inc(edges_padded, 1)
                G.memset(prev_i[:, :], -1).then_inc(edges_padded, 1)
                G.memset(xs[:, NT - 1, :], 0.0).then_inc(x_zeroed, 1)
                G.iota(iota_i[:, :], [[1, STEPS]], base=0, channel_multiplier=0).then_inc(consts_set, 1)
                G.iota(part_i[:, :], [[ER, EC]], base=0, channel_multiplier=1).then_inc(consts_set, 1)
                G.iota(step_i[:, :], [[SR, SC]], base=0, channel_multiplier=1).then_inc(consts_set, 1)
                G.iota(bound_i[:, :], [[P, NT - 1]], base=P, channel_multiplier=0).then_inc(consts_set, 1)
                G.iota(nt_i[:, :], [[1, NT - 1]], base=1, channel_multiplier=0).then_inc(consts_set, 1)
                G.iota(pcol_i[:, :], [[0, 1]], base=0, channel_multiplier=1).then_inc(consts_set, 1)
                G.memset(ones[:, :], 1.0).then_inc(consts_set, 1)
                G.memset(ident[:, :], 0.0).then_inc(masks_set, 1)
                pool.wait_ge(masks_set, 1)
                G.affine_select(out=ident[:, :], in_=ident[:, :], compare_op=ALU.not_equal, fill=1.0,
                                base=0, pattern=[[-1, P]], channel_multiplier=1).then_inc(masks_set, 1)
                G.memset(v_src[:, STEPS:STEPS + U], 0)
                G.memset(v_loc[:, STEPS:STEPS + U], -1.0)

            @block.scalar
            def _(act):
                act.wait_ge(edges_padded, 4)
                full = LAST_C * ER * P
                rest = (ET - 1) * P
                for n, arr in enumerate((src, dst)):
                    act.dma_start(e_int[:, n, 0:LAST_C, :], arr[0:full].rearrange("(c r e) -> r c e", r=ER, e=P)).then_inc(edges_in, 16)
                    act.dma_start(e_int[0:LAST_P, n, LAST_C, :], arr[full:rest].rearrange("(r e) -> r e", e=P)).then_inc(edges_in, 16)
                    act.dma_start(e_int[LAST_P:LAST_P + 1, n, LAST_C, 0:LAST_EDGES], arr[rest:E].unsqueeze(0)).then_inc(edges_in, 16)
                last_of = dst[0:rest].rearrange("(k e) -> k e", e=P)[:, P - 1:P]
                act.dma_start(prev_i[1:ER, 0:1], last_of[0:ER - 1, :], allow_slow_non_contiguous=True).then_inc(edges_in, 16)
                for c in range(1, EC):
                    act.dma_start(prev_i[:, c:c + 1], last_of[c * ER - 1:(c + 1) * ER - 1, :], allow_slow_non_contiguous=True).then_inc(edges_in, 16)
                wgt = edge_weight.rearrange("e o -> (e o)")
                act.dma_start(e_wgt[:, 0:LAST_C, :], wgt[0:full].rearrange("(c r e) -> r c e", r=ER, e=P)).then_inc(edges_in, 16)
                act.dma_start(e_wgt[0:LAST_P, LAST_C, :], wgt[full:rest].rearrange("(r e) -> r e", e=P)).then_inc(edges_in, 16)
                act.dma_start(e_wgt[LAST_P:LAST_P + 1, LAST_C, 0:LAST_EDGES], wgt[rest:E].unsqueeze(0)).then_inc(edges_in, 16)
                for c in range(2):
                    for half in range(2):
                        act.wait_ge(weightsT, 2 * c + half + 1)
                        A.copy(wT[:, c, half * 512:(half + 1) * 512], bank[2 * c + half][:, :]).then_inc(weights_copied, 1)
                for k in range(2):
                    act.wait_ge(weightsT, 5 + k)
                    A.copy(w1T[:, 2 * k:2 * k + 2, :], bank[4 + k][:, :].rearrange("p (k d) -> p k d", k=2)).then_inc(weights_copied, 1)
                act.wait_ge(x_in, 32)

            @block.tensor
            def _(pe):
                pe.wait_ge(masks_set, 2)
                pe.wait_ge(weights_in, 80)
                for c in range(2):
                    for half in range(2):
                        for b in range(4):
                            last = T_.transpose(bank[2 * c + half][:, b * P:(b + 1) * P], wnat[:, 4 * half + b, c * P:(c + 1) * P], ident[:, :])
                        last.then_inc(weightsT, 1)
                for k2 in range(2):
                    for k in range(2):
                        for b in range(2):
                            last = T_.transpose(bank[4 + k2][:, (2 * k + b) * P:(2 * k + b + 1) * P],
                                                w1nat[:, b, (2 * k2 + k) * P:(2 * k2 + k + 1) * P], ident[:, :])
                    last.then_inc(weightsT, 1)
                pe.wait_ge(below_ready, 1)
                for c in range(EC):
                    last = T_.matmul(bank[6][:, 0:NT - 1], ones[0:ER, :], below[:, :, c], start=(c == 0), stop=(c == EC - 1))
                last.then_inc(below_summed, 1)
                pe.wait_ge(tcol_ready, 1)
                for c in range(SC):
                    last = T_.matmul(bank[7][:, c * SR:(c + 1) * SR], tcol_bc[:, c, :], ident[0:SR, 0:SR], start=True, stop=True)
                last.then_inc(trow_summed, 1)
                pe.wait_ge(sel_ready, 1)
                pe.wait_ge(weights_copied, 6)
                for n, what in enumerate((e_dst, e_src, e_wgt)):
                    for c in range(EC):
                        last = T_.matmul(bank[n][:, 0:STEPS], what[:, c, :], sel[:, c, :], start=(c == 0), stop=(c == EC - 1))
                for n, what in enumerate((e_dst, e_start)):
                    for sc in range(SC):
                        for c in range(EC):
                            last = T_.matmul(bank[3 + n][0:SR, sc * P:(sc + 1) * P], sel[:, c, sc * SR:(sc + 1) * SR], what[:, c, :],
                                             start=(c == 0), stop=(c == EC - 1))
                last.then_inc(picked, 1)

            @block.vector
            def _(dve):
                chain = Chain(dve, "index_chain")
                f = chain.follow
                dve.wait_ge(consts_set, 7)
                V.tensor_copy(iota_f[:, :], iota_i[:, :])
                V.tensor_copy(part_f[:, :], part_i[:, :])
                V.tensor_copy(step_f[:, :], step_i[:, :])
                V.tensor_copy(bound_f[:, :], bound_i[:, :])
                V.tensor_copy(pcol[:, :], pcol_i[:, :])
                f(V.tensor_copy(nt_f[:, :], nt_i[:, :]))
                dve.wait_ge(edges_in, 13 * 16)
                V.tensor_copy(e_src[:, :, :], e_int[:, 0, :, :])
                V.tensor_copy(e_dst[:, :, :], e_int[:, 1, :, :])
                f(V.tensor_copy(prev_f[:, :], prev_i[:, :]))
                V.tensor_tensor(e_start[:, :, 1:P], e_dst[:, :, 1:P], e_dst[:, :, 0:P - 1], ALU.not_equal)
                V.tensor_tensor(e_start[:, :, 0], e_dst[:, :, 0], prev_f[:, :], ALU.not_equal)
                V.tensor_tensor(below[:, :, :], bound_f[0:ER, :].unsqueeze(2).to_broadcast([ER, NT - 1, EC]),
                                e_dst[:, :, P - 1].unsqueeze(1).to_broadcast([ER, NT - 1, EC]), ALU.is_gt).then_inc(below_ready, 1)
                dve.wait_ge(below_summed, 1)
                f(V.tensor_tensor(turn[:, :], bank[6][:, 0:NT - 1], nt_f[:, :], ALU.add))
                f(V.tensor_tensor(reached[:, :, :], step_f[0:SR, :].unsqueeze(2).to_broadcast([SR, SC, NT - 1]),
                                  turn[0:SR, :].unsqueeze(1).to_broadcast([SR, SC, NT - 1]), ALU.is_ge))
                f(V.tensor_reduce(tcol[:, :], reached[:, :, :], AX.X, ALU.add))
                V.tensor_copy(tcol_bc[:, :, :], tcol[:, :].unsqueeze(2).to_broadcast([SR, SC, P])).then_inc(tcol_ready, 1)
                dve.wait_ge(trow_summed, 1)
                f(V.tensor_copy(t_row[:, :], bank[7][:, 0:STEPS]))
                V.tensor_copy(t_int[:, :], t_row[0:1, :])
                f(V.tensor_tensor(r_row[:, :], iota_f[:, :], t_row[:, :], ALU.subtract))
                for c in range(EC):
                    last = V.tensor_scalar(sel[:, c, :], r_row[0:ER, :], part_f[0:ER, c:c + 1], None, ALU.is_equal)
                last.then_inc(sel_ready, 1)
                dve.wait_ge(picked, 1)
                V.tensor_copy(v_src[:, 0:STEPS], bank[1][:, 0:STEPS])
                V.tensor_copy(v_wgt[:, :], bank[2][:, 0:STEPS])
                f(V.scalar_tensor_tensor(v_loc[:, 0:STEPS], t_row[:, :], float(-P), bank[0][:, 0:STEPS], ALU.mult, ALU.add))
                f(V.tensor_scalar(v_loc[:, 0:STEPS], v_loc[:, 0:STEPS], -1.0, float(P), ALU.max, ALU.min))
                V.tensor_scalar(r_row[:, :], v_loc[:, 0:STEPS], 0.0, NEG, ALU.is_lt, ALU.mult)
                f(V.tensor_scalar(maskb[:, :], v_loc[:, 0:STEPS], float(P), NEG, ALU.is_ge, ALU.mult))
                V.tensor_tensor(maskb[:, :], maskb[:, :], r_row[:, :], ALU.add)
                f(V.tensor_scalar(tcol[:, :], tcol[:, :], float(P), None, ALU.mult))
                for sc in range(SC):
                    last = V.tensor_scalar(row_loc[:, sc, :], bank[3][0:SR, sc * P:(sc + 1) * P], tcol[:, sc:sc + 1], None, ALU.subtract)
                f(last)
                f(V.tensor_scalar(row_loc[:, :, :], row_loc[:, :, :], -1.0, float(P), ALU.max, ALU.min))
                V.tensor_copy(row_loc_b[:, :, :], row_loc[:, :, :]).then_inc(local_ready, 1)
                V.tensor_scalar(row_in[:, :, :], row_loc[:, :, :], 0.0, NEG, ALU.is_ge, ALU.mult)
                f(V.tensor_scalar(row_start[:, :, :], row_loc[:, :, :], float(P), None, ALU.is_lt))
                f(V.tensor_tensor(row_in[:, :, :], row_in[:, :, :], row_start[:, :, :], ALU.mult))
                V.tensor_tensor(row_start[:, :, :], row_in[:, :, :],
                                bank[4][0:SR, :].rearrange("p (c e) -> p c e", c=SC), ALU.mult)

        stage.close()
        h_buf = tb("h_buf", [P, 2, D])
        hT = tb("hT", [P, 2, 2, P])
        qv_out = tb("qv_out", [P, 2, 2 * D])
        def moments(f):
            m0, v0, m1, v1 = stats[:, :, 1], stats[:, :, 2], stats[:, :, 4], stats[:, :, 5]
            V.tensor_tensor(t_a[:, :], m0, m1, ALU.subtract)
            V.tensor_tensor(mean[:, :], m0, m1, ALU.add)
            f(V.tensor_tensor(t_b[:, :], v0, v1, ALU.add))
            f(V.tensor_tensor(t_a[:, :], t_a[:, :], t_a[:, :], ALU.mult))
            V.tensor_scalar(mean[:, :], mean[:, :], 0.5, None, ALU.mult)
            V.tensor_scalar(t_a[:, :], t_a[:, :], 0.25, None, ALU.mult)
            f(V.tensor_scalar(t_b[:, :], t_b[:, :], 1.0 / D, 1e-5, ALU.mult, ALU.add))
            f(V.tensor_tensor(t_b[:, :], t_b[:, :], t_a[:, :], ALU.add))

        def pairs(eng, body):
            with eng.Fori(0, NT // 2) as i:
                body(i * 2, i, 0, False)
                body(i * 2 + 1, i, 1, False)
            body(NT - 1, NT // 2, 0, True)

        with nc.Block() as block:
            var_ready, root_ready, norm_ready = sem("var_ready"), sem("root_ready"), sem("norm_ready")
            h_ready, h_turned, hT_ready = sem("h_ready"), sem("h_turned"), sem("hT_ready")
            proj_done, proj_read, rows_ready = sem("proj_done"), sem("proj_read"), sem("rows_ready")
            rows_stored = [sem("rows_stored0"), sem("rows_stored1")]

            @block.vector
            def _(dve):
                f = Chain(dve, "norm_chain").follow
                with dve.Fori(0, NT) as T:
                    V.bn_stats(stats[:, bass.ds(T, 1), :], xs[:, bass.ds(T, 1), :])
                f(V.tensor_tensor(gate_u[:, :], gate[:, 0:D], gate[:, 2 * D:3 * D], ALU.add))
                moments(f)
                V.tensor_tensor(gate_w[:, :], gate[:, 0:D], gate[:, D:2 * D], ALU.add).then_inc(var_ready, 1)
                dve.wait_ge(root_ready, 1)
                f(V.reciprocal(rstd[:, :], t_a[:, :]))
                V.scalar_tensor_tensor(shift[:, :], mean[:, :], -1.0, rstd[:, :], ALU.mult, ALU.mult).then_inc(norm_ready, 1)
                dve.sem_inc(proj_read, 2)
                dve.sem_inc(rows_stored[0], 16)
                dve.sem_inc(rows_stored[1], 16)

                def body(T, i, b, last):
                    dve.wait_ge(proj_done, T * 2 + 1)
                    dve.wait_ge(rows_stored[b], i * 16 + 16)
                    V.tensor_tensor(qv_out[:, b, :], bank[2 + 2 * b][:, :], bias[:, 0:2 * D], ALU.add).then_inc(rows_ready, 1)
                    dve.wait_ge(proj_done, T * 2 + 2)
                    V.tensor_tensor(ks[:, bass.ds(T, 1), :, :].rearrange("p o k d -> p (o k d)"), bank[3 + 2 * b][:, :],
                                    bias[:, 2 * D:4 * D], ALU.add).then_inc(proj_read, 1)
                pairs(dve, body)

            @block.scalar
            def _(act):
                act.wait_ge(var_ready, 1)
                A.sqrt(t_a[:, :], t_b[:, :]).then_inc(root_ready, 1)
                act.wait_ge(norm_ready, 1)

                def normalise(T, b):
                    A.activation(h_buf[:, b, :], xs[:, bass.ds(T, 1), :].rearrange("p o d -> p (o d)"), ACT.Relu,
                                 bias=shift[:, bass.ds(T, 1)], scale=rstd[:, bass.ds(T, 1)]).then_inc(h_ready, 1)
                act.sem_inc(hT_ready, 1)
                act.sem_inc(h_turned, 1)
                normalise(0, 0)

                def body(T, i, b, last):
                    if not last:
                        act.wait_ge(h_turned, T + 1)
                        normalise(T + 1, 1 - b)
                    act.wait_ge(h_turned, T + 2)
                    A.copy(hT[:, b, :, :].rearrange("p c n -> p (c n)"), bank[b][:, 0:2 * P]).then_inc(hT_ready, 1)
                pairs(act, body)

            @block.tensor
            def _(pe):
                def turn_h(b):
                    for c in range(2):
                        last = T_.transpose(bank[b][:, c * P:(c + 1) * P], h_buf[:, b, c * P:(c + 1) * P], ident[:, :])
                    last.then_inc(h_turned, 1)
                pe.wait_ge(h_ready, 1)
                turn_h(0)

                def body(T, i, b, last):
                    if not last:
                        pe.wait_ge(h_ready, T + 2)
                        pe.wait_ge(hT_ready, T + 1)
                        turn_h(1 - b)
                    pe.wait_ge(hT_ready, T + 2)
                    pe.wait_ge(proj_read, T + 1)
                    for half in range(2):
                        for c in range(2):
                            mm = T_.matmul(bank[2 + 2 * b + half][:, :], hT[:, b, c, :], wT[:, c, half * 512:(half + 1) * 512],
                                           start=(c == 0), stop=(c == 1))
                        mm.then_inc(proj_done, 1)
                pairs(pe, body)

            @block.sync
            def _(sp):
                def body(T, i, b, last):
                    sp.wait_ge(rows_ready, T + 1)
                    sp.dma_start(qv_tab[bass.ds(T * P, P), :], qv_out[:, b, :]).then_inc(rows_stored[b], 16)
                pairs(sp, body)
                sp.wait_ge(rows_stored[0], 16 * (NT // 2 + 1) + 16)
                sp.wait_ge(rows_stored[1], 16 * (NT // 2) + 16)

        def gather_rows(tag, table, ring, slots_free):
            got = [sem(f"{tag}_got{u}") for u in range(U)]
            index_ready, claimed = sem(f"{tag}_index_ready"), sem(f"{tag}_claimed")
            H = U // 2

            def pool_part(pool):
                with pool.Fori(0, ITERS) as i:
                    for u in range(U):
                        if u % H == 0:
                            pool.wait_ge(index_ready, i * 2 + (1 + u // H))
                            pool.sem_inc(claimed, 1)
                        for signal, per, level in slots_free(u):
                            pool.wait_ge(signal, i * per + level)
                            pool.sem_inc(claimed, 1)
                        pool.indirect_dma_start(ring(u), None, table,
                                                bass.IndirectOffsetOnAxis(ap=src_stage[:, u:u + 1], axis=0)).then_inc(got[u], 16)

            def index_first(act):
                for half in range(2):
                    A.copy(src_stage[:, half * H:(half + 1) * H], v_src[:, half * H:(half + 1) * H]).then_inc(index_ready, 1)

            def index_next(act, i):
                for half in range(2):
                    for u in range(H):
                        act.wait_ge(got[half * H + u], i * 16 + 16)
                    A.copy(src_stage[:, half * H:(half + 1) * H], v_src[:, bass.ds(i * U + (U + half * H), H)]).then_inc(index_ready, 1)
            return got, pool_part, index_first, index_next

        def load_node_tiles(eng, i):
            _, vals = nc.values_load_multi_w_load_instructions(t_int[0:1, bass.ds(i * U, U)], engines=[eng.engine],
                                                               min_val=0, max_val=NT - 1, skip_runtime_bounds_check_because='T(t) is clamped by its construction')
            return vals

        stage.close()
        proj.close()
        H = U // 2
        Q = 4
        qv_ring = tb("qv_ring", [P, U, 2 * D])
        loc_bc = tb("loc_bc", [P, 2, H * P], BF16)
        hotT = tb("hotT", [P, 2, H, P])
        prod = tb("prod", [P, H, D])
        assert H % 5 == 0 and U % Q == 0
        with nc.Block() as block:
            loc_in = [sem("loc_in0"), sem("loc_in1")]
            hotT_ready, k_spread, qk_used = sem("hotT_ready"), sem("k_spread"), sem("qk_used")
            v_stored = [sem(f"v_stored{n}") for n in range(U // Q)]
            got, pool_part, index_first, index_next = gather_rows(
                "qv", qv_tab, lambda u: qv_ring[:, u, :],
                lambda u: [(qk_used, H, u // 2 + 1)] * (u % 2 == 0) + [(v_stored[u // Q], 16, 16)] * (u % Q == 0))

            @block.gpsimd
            def _(pool):
                for n in range(U // Q):
                    pool.sem_inc(v_stored[n], 16)
                pool_part(pool)

            @block.scalar
            def _(act):
                index_first(act)
                with act.Fori(0, ITERS) as i:
                    index_next(act, i)

            @block.sync
            def _(sp):
                def load_locals(half, step):
                    sp.dma_start(loc_bc[:, half, :], local_tab[bass.ds(step, H), :].rearrange("t e -> (t e)").partition_broadcast(P)).then_inc(loc_in[half], 16)
                load_locals(0, 0)
                load_locals(1, H)
                with sp.Fori(0, ITERS) as i:
                    for n in range(U // Q):
                        if n == 1 or n == 3:
                            half = n // 2
                            sp.wait_ge(hotT_ready, i * 2 + (1 + half))
                            load_locals(half, i * U + (U + half * H))
                        for u in range(n * Q, (n + 1) * Q):
                            sp.wait_ge(got[u], i * 16 + 16)
                        sp.dma_start(v_rows[bass.ds(i * U + n * Q, Q), :, :].rearrange("t p d -> p t d"), qv_ring[:, n * Q:(n + 1) * Q, D:2 * D]).then_inc(v_stored[n], 16)
                for half in range(2):
                    sp.wait_ge(loc_in[half], 16 * (ITERS + 1))
                for n in range(U // Q):
                    sp.wait_ge(v_stored[n], 16 * (ITERS + 1))

            @block.tensor
            def _(pe):
                with pe.Fori(0, ITERS) as i:
                    tiles = load_node_tiles(pe, i)
                    for half in range(2):
                        pe.wait_ge(hotT_ready, i * 2 + (1 + half))
                        for j in range(H // 2):
                            pe.wait_ge(qk_used, i * H + (half * (H // 2) + j + 6))
                            for u in (2 * j, 2 * j + 1):
                                mm = T_.matmul(bank[j][:, (u % 2) * D:(u % 2 + 1) * D], hotT[:, half, u, :],
                                               ks[:, bass.ds(tiles[half * H + u], 1), 0, :], start=True, stop=True)
                            mm.then_inc(k_spread, 1)

            @block.vector
            def _(dve):
                dve.sem_inc(qk_used, H)

                def build(half, level):
                    dve.wait_ge(loc_in[half], level)
                    V.tensor_scalar(hotT[:, half, :, :].rearrange("p u e -> p (u e)"), loc_bc[:, half, :], pcol[:, 0:1], None,
                                    ALU.is_equal).then_inc(hotT_ready, 1)

                def multiply(i, half):
                    for j in range(H // 2):
                        m = half * (H // 2) + j
                        dve.wait_ge(k_spread, i * H + (m + 1))
                        dve.wait_ge(got[2 * m], i * 16 + 16)
                        dve.wait_ge(got[2 * m + 1], i * 16 + 16)
                        V.tensor_tensor(prod[:, 2 * j:2 * j + 2, :], qv_ring[:, 2 * m:2 * m + 2, 0:D],
                                        bank[j][:, :].rearrange("p (u d) -> p u d", u=2), ALU.mult).then_inc(qk_used, 1)
                    dve.wait_ge(qk_used, i * H + (H + (half + 1) * (H // 2)))
                    V.tensor_reduce(score[:, bass.ds(i * (U * HEADS) + half * H * HEADS, H * HEADS)],
                                    prod[:, :, :].rearrange("p u (h d) -> p (u h) d", h=HEADS), AX.X, ALU.add).then_inc(summed, 1)
                    dve.wait_ge(summed, i * 2 + (1 + half))
                summed = sem("summed")
                build(0, 16)
                with dve.Fori(0, ITERS) as i:
                    build(1, i * 16 + 16)
                    multiply(i, 0)
                    build(0, i * 16 + 32)
                    multiply(i, 1)

        stage.close()
        seg = tb("seg", [SR, SC, HEADS, P])
        seg2 = tb("seg2", [SR, SC, HEADS, P])
        cuts = tb("cuts", [SR, SC, HEADS, P])
        reach = tb("reach", [SR, SC, P])
        cut_all = tb("cut_all", [SR, SC])
        ends = tb("ends", [SR, SC, 2, HEADS])
        firsts = tb("firsts", [SR, SC, HEADS])
        head_ends = tb("head_ends", [HEADS, STEPS])
        head_cuts = tb("head_cuts", [HEADS, STEPS])
        head_first = tb("head_first", [HEADS, STEPS])
        back_cuts = tb("back_cuts", [HEADS, STEPS])
        carry = tb("carry", [HEADS, STEPS + 1])
        carry_in = tb("carry_in", [HEADS, STEPS])
        carry_col = tb("carry_col", [SR, SC, HEADS])

        with nc.Block() as block:
            masked, rows_turned, rows_copied = sem("masked"), sem("rows_turned"), sem("rows_copied")
            ends_ready, ends_turned, carry_ready, carry_turned = sem("ends_ready"), sem("ends_turned"), sem("carry_ready"), sem("carry_turned")
            max_ready, max_turned, shifted = sem("max_ready"), sem("max_turned"), sem("shifted")
            by_step = score[:, :].rearrange("p (t h) -> p t h", h=HEADS)

            @block.tensor
            def _(pe):
                pe.wait_ge(masked, 1)
                for sc in range(SC):
                    for h in range(HEADS):
                        last = T_.transpose(bank[sc][0:SR, h * P:(h + 1) * P], by_step[:, sc * SR:(sc + 1) * SR, h], ident[:, :])
                    last.then_inc(rows_turned, 1)
                pe.wait_ge(ends_ready, 1)
                for sc in range(SC):
                    T_.transpose(bank[7][0:HEADS, sc * SR:(sc + 1) * SR], firsts[:, sc, :], ident[0:SR, 0:SR])
                for way in range(2):
                    pe.wait_ge(ends_ready, way + 1)
                    for sc in range(SC):
                        T_.transpose(bank[4][0:HEADS, sc * SR:(sc + 1) * SR], ends[:, sc, 0, :], ident[0:SR, 0:SR])
                        last = T_.transpose(bank[5][0:HEADS, sc * SR:(sc + 1) * SR], ends[:, sc, 1, :], ident[0:SR, 0:SR])
                    last.then_inc(ends_turned, 1)
                    pe.wait_ge(carry_ready, way + 1)
                    for sc in range(SC):
                        last = T_.transpose(bank[6][0:SR, sc * HEADS:(sc + 1) * HEADS], carry_in[:, sc * SR:(sc + 1) * SR],
                                            ident[0:HEADS, 0:HEADS])
                    last.then_inc(carry_turned, 1)
                for h in range(HEADS):
                    for sc in range(SC):
                        if h == 0:
                            pe.wait_ge(max_ready, sc + 1)
                        last = T_.transpose(bank[h][:, sc * SR:(sc + 1) * SR], seg[:, sc, h, :], ident[0:SR, 0:SR])
                    last.then_inc(max_turned, 1)

            @block.scalar
            def _(act):
                for sc in range(SC):
                    act.wait_ge(rows_turned, sc + 1)
                    A.copy(seg[:, sc, :, :].rearrange("p h e -> p (h e)"), bank[sc][0:SR, :]).then_inc(rows_copied, 1)
                act.wait_ge(shifted, HEADS)
                A.activation(score[:, :], score[:, :], ACT.Exp, scale=SCALE)

            @block.vector
            def _(dve):
                chain = Chain(dve, "max_chain")
                f = chain.follow

                def rows(t, sc):
                    return t[:, sc, :, :].rearrange("p h e -> p (h e)")

                V.tensor_tensor(by_step, by_step, maskb[:, :].unsqueeze(2).to_broadcast([P, STEPS, HEADS]), ALU.add).then_inc(masked, 1)
                f(V.tensor_copy(cuts[:, :, :, :], row_start[:, :, :].unsqueeze(2).to_broadcast([SR, SC, HEADS, P])))
                f(V.memset(cuts[:, :, :, 0], NEG))
                for sc in range(SC):
                    dve.wait_ge(rows_copied, sc + 1)
                    V.tensor_tensor_scan(rows(seg2, sc), rows(cuts, sc), rows(seg, sc), NEG, ALU.add, ALU.max)
                for sc in range(SC):
                    V.tensor_tensor_scan(reach[:, sc, :], row_start[:, sc, :], row_start[:, sc, :], 0.0, ALU.min, ALU.min)
                f(V.tensor_reduce(cut_all[:, :], row_start[:, :, :], AX.X, ALU.min))
                V.tensor_copy(firsts[:, :, :], row_start[:, :, 0].unsqueeze(2).to_broadcast([SR, SC, HEADS]))
                V.tensor_copy(ends[:, :, 0, :], seg2[:, :, :, P - 1])
                V.tensor_copy(ends[:, :, 1, :], cut_all[:, :].unsqueeze(2).to_broadcast([SR, SC, HEADS])).then_inc(ends_ready, 1)
                dve.wait_ge(ends_turned, 1)
                V.tensor_copy(head_ends[:, :], bank[4][0:HEADS, 0:STEPS])
                V.tensor_copy(head_cuts[:, :], bank[5][0:HEADS, 0:STEPS])
                V.tensor_copy(head_first[:, :], bank[7][0:HEADS, 0:STEPS])
                f(V.memset(carry[:, :], NEG))
                f(V.tensor_tensor_scan(carry[:, 1:STEPS + 1], head_cuts[:, :], head_ends[:, :], NEG, ALU.add, ALU.max))
                V.tensor_copy(carry_in[:, :], carry[:, 0:STEPS]).then_inc(carry_ready, 1)
                dve.wait_ge(carry_turned, 1)
                f(V.tensor_copy(carry_col[:, :, :], bank[6][0:SR, 0:SC * HEADS].rearrange("p (c h) -> p c h", c=SC)))
                for sc in range(SC):
                    for h in range(HEADS):
                        last = V.scalar_tensor_tensor(seg2[:, sc, h, :], reach[:, sc, :], carry_col[:, sc, h:h + 1], seg2[:, sc, h, :], ALU.add, ALU.max)
                f(last)
                V.memset(cuts[:, :, :, P - 1], NEG)
                f(V.tensor_copy(cuts[:, :, :, 0:P - 1], row_start[:, :, 1:P].unsqueeze(2).to_broadcast([SR, SC, HEADS, P - 1])))
                for sc in range(SC):
                    last = V.tensor_tensor_scan(rows(seg, sc)[:, ::-1], rows(cuts, sc)[:, ::-1], rows(seg2, sc)[:, ::-1], NEG, ALU.add, ALU.max)
                f(last)
                f(V.memset(cuts[:, :, 0, P - 1], 0.0))
                for sc in range(SC):
                    V.tensor_tensor_scan(reach[:, sc, ::-1], cuts[:, sc, 0, ::-1], cuts[:, sc, 0, ::-1], 0.0, ALU.min, ALU.min)
                f(V.tensor_copy(ends[:, :, 0, :], seg[:, :, :, 0]))
                V.tensor_copy(ends[:, :, 1, :], reach[:, :, 0].unsqueeze(2).to_broadcast([SR, SC, HEADS])).then_inc(ends_ready, 1)
                dve.wait_ge(ends_turned, 2)
                V.tensor_copy(head_ends[:, :], bank[4][0:HEADS, 0:STEPS])
                V.tensor_copy(head_cuts[:, :], bank[5][0:HEADS, 0:STEPS])
                f(V.memset(carry_in[:, :], NEG))
                f(V.tensor_tensor(back_cuts[:, 0:STEPS - 1], head_cuts[:, 0:STEPS - 1], head_first[:, 1:STEPS], ALU.add))
                f(V.memset(back_cuts[:, STEPS - 1:STEPS], NEG))
                f(V.tensor_tensor_scan(carry[:, 0:STEPS][:, ::-1], back_cuts[:, ::-1], head_ends[:, ::-1], NEG, ALU.add, ALU.max))
                V.tensor_tensor(carry_in[:, 0:STEPS - 1], carry[:, 1:STEPS], head_first[:, 1:STEPS], ALU.add).then_inc(carry_ready, 1)
                dve.wait_ge(carry_turned, 2)
                f(V.tensor_copy(carry_col[:, :, :], bank[6][0:SR, 0:SC * HEADS].rearrange("p (c h) -> p c h", c=SC)))
                for sc in range(SC):
                    for h in range(HEADS):
                        last = V.scalar_tensor_tensor(seg[:, sc, h, :], reach[:, sc, :], carry_col[:, sc, h:h + 1], seg[:, sc, h, :], ALU.add, ALU.max)
                    last.then_inc(max_ready, 1)
                for h in range(HEADS):
                    dve.wait_ge(max_turned, h + 1)
                    V.tensor_tensor(by_step[:, :, h], by_step[:, :, h], bank[h][:, 0:STEPS], ALU.subtract).then_inc(shifted, 1)

        stage.close()
        acc = sb("acc", [P, NT, AW])
        NQ = U // Q
        acc_odd = tb("acc_odd", [P, NT, AW])
        ring = tb("ring", [P, U, AW])
        hot = tb("hot", [P, U, P])
        by_act = [u for u in range(U) if u % Q in (0, 1)]
        with nc.Block() as block:
            sums_done, sums_added, hot_ready, ex_ready = sem("sums_done"), sem("sums_added"), sem("hot_ready"), sem("ex_ready")
            by_act_done, by_pool_done, ones_set, acc_zeroed = sem("by_act_done"), sem("by_pool_done"), sem("ones_set"), sem("acc_zeroed")
            v_in = [sem(f"v_in{n}") for n in range(NQ)]

            @block.sync
            def _(sp):
                sp.wait_ge(ones_set, 1)
                with sp.Fori(0, ITERS) as i:
                    for n in range(NQ):
                        sp.wait_ge(sums_done, i * U + (n + 1) * Q)
                        sp.dma_start(ring[:, n * Q:(n + 1) * Q, 0:D], v_rows[bass.ds(i * U + n * Q, Q), :, :].rearrange("t p d -> p t d")).then_inc(v_in[n], 16)

            def weighted(t, u):
                return t[:, u, 0:D].rearrange("p (h d) -> p h d", h=HEADS)

            @block.gpsimd
            def _(pool):
                G.memset(ring[:, :, :], 1.0).then_inc(ones_set, 1)
                G.memset(acc[:, :, :], 0.0).then_inc(acc_zeroed, 1)
                G.memset(acc_odd[:, :, :], 0.0).then_inc(acc_zeroed, 1)
                with pool.Fori(0, ITERS) as i:
                    for n in range(NQ):
                        pool.wait_ge(v_in[n], i * 16 + 16)
                        pool.sem_inc(passed, 1)
                        u = n * Q + 2
                        r = ring[:, u:u + 2, 0:D].rearrange("p u (h d) -> p u h d", h=HEADS)
                        G.tensor_tensor(r, r, score[:, bass.ds(i * (U * HEADS) + u * HEADS, 2 * HEADS)].rearrange("p (u h) -> p u h", u=2)
                                        .unsqueeze(3).to_broadcast([P, 2, HEADS, DH]), ALU.mult).then_inc(by_pool_done, 1)

            @block.scalar
            def _(act):
                with act.Fori(0, ITERS) as i:
                    for n in range(NQ):
                        act.wait_ge(v_in[n], i * 16 + 16)
                        act.sem_inc(passed2, 1)
                        A.copy(ring[:, n * Q:(n + 1) * Q, DEN:DEN + HEADS], score[:, bass.ds(i * (U * HEADS) + n * Q * HEADS, Q * HEADS)].rearrange("p (u h) -> p u h", u=Q)).then_inc(ex_ready, 1)
                        for u in (n * Q, n * Q + 1):
                            for h in range(HEADS):
                                part = ring[:, u, h * DH:(h + 1) * DH]
                                last = A.activation(part, part, ACT.Copy, scale=score[:, bass.ds(i * (U * HEADS) + u * HEADS + h, 1)])
                            last.then_inc(by_act_done, 1)

            @block.tensor
            def _(pe):
                pe.sem_inc(sums_done, U)
                with pe.Fori(0, ITERS) as i:
                    for u in range(U):
                        if u % Q == 0:
                            pe.wait_ge(ex_ready, i * NQ + (u // Q + 1))
                            pe.wait_ge(hot_ready, i * NQ + (u // Q + 1))
                        if u % Q < 2:
                            pe.wait_ge(by_act_done, i * (2 * NQ) + (u // Q * 2 + u % Q + 1))
                        elif u % Q == 2:
                            pe.wait_ge(by_pool_done, i * NQ + (u // Q + 1))
                        pe.wait_ge(sums_added, i * U + (u + 1))
                        T_.matmul(bank[u % 4][:, 0:DEG + 1], hot[:, u, :], ring[:, u, 0:DEG + 1], start=True, stop=True).then_inc(sums_done, 1)

            @block.vector
            def _(dve):
                dve.wait_ge(acc_zeroed, 2)
                dve.sem_inc(sums_added, 4)

                def build(n, first):
                    V.tensor_tensor(hot[:, n * Q:(n + 1) * Q, :], iota_f[:, 0:P].unsqueeze(1).to_broadcast([P, Q, P]),
                                    v_loc[:, first].unsqueeze(2).to_broadcast([P, Q, P]), ALU.is_equal).then_inc(hot_ready, 1)
                build(0, slice(0, Q))
                with dve.Fori(0, ITERS) as i:
                    tiles = load_node_tiles(dve, i)
                    for n in range(NQ):
                        if n < NQ - 1:
                            build(n + 1, bass.ds(i * U + (n + 1) * Q, Q))
                        else:
                            build(0, bass.ds(i * U + U, Q))
                        for u in range(n * Q, (n + 1) * Q):
                            dve.wait_ge(sums_done, i * U + (U + u + 1))
                            dve.wait_ge(sums_added, i * U + (4 + u - 1))
                            a = (acc, acc_odd)[u % 2][:, bass.ds(tiles[u], 1), 0:DEG + 1].rearrange("p o d -> p (o d)")
                            V.tensor_tensor(a, a, bank[u % 4][:, 0:DEG + 1], ALU.add).then_inc(sums_added, 1)
                dve.wait_ge(sums_added, STEPS + 4)
                V.tensor_tensor(acc[:, :, :], acc[:, :, :], acc_odd[:, :, :], ALU.add)

        stage.close()
        sA = tb("sA", [P, NB, D])
        sB = tb("sB", [P, NB, D])
        sC = tb("sC", [P, NB, D])
        with nc.Block() as block:
            z_ready, e_ready, var_ready, root_ready, relu_ready, relu_used, neg_used = [sem("mid_" + n) for n in "z e var root relu relu_used neg_used".split()]
            norm2_ready, h2_ready, h2_stored = sem("norm2_ready"), sem("h2_ready"), sem("h2_stored")
            normed, normed_used = sem("normed"), sem("normed_used")

            def grp(t, g, lo=0, n=D):
                return t[:, bass.ds(g * NB, NB), lo:lo + n]

            @block.vector
            def _(dve):
                chain = Chain(dve, "between_chain")
                f = chain.follow
                f(V.tensor_scalar(rden[:, :, :], acc[:, :, DEN:DEN + HEADS], 1e-30, None, ALU.max))
                V.reciprocal(rden[:, :, :], rden[:, :, :])
                f(V.tensor_scalar(rdeg[:, :], acc[:, :, DEG], 1.0, None, ALU.max))
                f(V.reciprocal(rdeg[:, :], rdeg[:, :]))
                with dve.Fori(0, NG) as g:
                    chain.enter(g, 5)
                    mean_v = grp(acc, g)
                    f(V.tensor_tensor(mean_v.rearrange("p t (h d) -> p t h d", h=HEADS), mean_v.rearrange("p t (h d) -> p t h d", h=HEADS),
                                      rden[:, bass.ds(g * NB, NB), :].unsqueeze(3).to_broadcast([P, NB, HEADS, DH]), ALU.mult))
                    skip_v = ks[:, bass.ds(g * NB, NB), 1, :]
                    f(V.tensor_tensor(skip_v, skip_v, mean_v, ALU.subtract))
                    V.tensor_tensor(sA[:, :, :], skip_v, gate_u[:, :].unsqueeze(1).to_broadcast([P, NB, D]), ALU.mult)
                    f(V.tensor_tensor(sB[:, :, :], mean_v, gate_w[:, :].unsqueeze(1).to_broadcast([P, NB, D]), ALU.mult))
                    f(V.tensor_tensor(sA[:, :, :], sA[:, :, :], sB[:, :, :], ALU.add))
                    f(V.tensor_reduce(zz[:, bass.ds(g * NB, NB)], sA[:, :, :], AX.X, ALU.add))
                chain.leave(NG)
                V.tensor_scalar(zz[:, :], zz[:, :], bg[:, 0:1], None, ALU.add).then_inc(z_ready, 1)
                dve.wait_ge(e_ready, 1)
                f(V.tensor_scalar(zz[:, :], zz[:, :], 1.0, None, ALU.add))
                f(V.reciprocal(zz[:, :], zz[:, :]))
                with dve.Fori(0, NG) as g:
                    chain.enter(g, 3)
                    f(V.tensor_tensor(sA[:, :, :], ks[:, bass.ds(g * NB, NB), 1, :], zz[:, bass.ds(g * NB, NB)].unsqueeze(2).to_broadcast([P, NB, D]), ALU.mult))
                    f(V.tensor_tensor(grp(acc, g), grp(acc, g), sA[:, :, :], ALU.add))
                    chain.pass_wait()
                    for n in range(NB):
                        last = V.bn_stats(stats[:, bass.ds(g * NB + n, 1), :], acc[:, bass.ds(g * NB + n, 1), 0:D])
                    f(last)
                chain.leave(NG)
                moments(f)
                V.tensor_copy(sA[:, 0, 0:1], sA[:, 0, 0:1]).then_inc(var_ready, 1)
                dve.wait_ge(root_ready, 1)
                f(V.reciprocal(rstd[:, :], t_a[:, :]))
                V.scalar_tensor_tensor(shift[:, :], mean[:, :], -1.0, rstd[:, :], ALU.mult, ALU.mult).then_inc(norm2_ready, 1)
                with dve.Fori(0, NG) as g:
                    chain.enter(g, 6)
                    dve.wait_ge(normed, g * NB + NB)
                    f(V.tensor_tensor(sA[:, :, :], grp(acc, g), lnw[:, :].unsqueeze(1).to_broadcast([P, NB, D]), ALU.mult))
                    f(V.tensor_tensor(sA[:, :, :], sA[:, :, :], lnb[:, :].unsqueeze(1).to_broadcast([P, NB, D]), ALU.add))
                    V.tensor_scalar(sB[:, :, :], sA[:, :, :], 0.0, pa[:, 0:1], ALU.min, ALU.mult)
                    f(V.tensor_scalar(sC[:, :, :], sA[:, :, :], 0.0, None, ALU.max))
                    f(V.tensor_tensor(sB[:, :, :], sB[:, :, :], sC[:, :, :], ALU.add))
                    f(V.tensor_tensor(grp(xs, g), grp(xs, g), sB[:, :, :], ALU.add))
                    chain.pass_wait()
                    for n in range(NB):
                        last = V.bn_stats(stats[:, bass.ds(g * NB + n, 1), :], xs[:, bass.ds(g * NB + n, 1), :])
                    f(last)
                chain.leave(NG)
                moments(f)
                V.tensor_copy(sA[:, 0, 0:1], sA[:, 0, 0:1]).then_inc(var_ready, 1)
                dve.wait_ge(root_ready, 2)
                f(V.reciprocal(rstd[:, :], t_a[:, :]))
                V.scalar_tensor_tensor(shift[:, :], mean[:, :], -1.0, rstd[:, :], ALU.mult, ALU.mult).then_inc(norm2_ready, 1)

            @block.scalar
            def _(act):
                act.wait_ge(z_ready, 1)
                A.activation(zz[:, :], zz[:, :], ACT.Exp, scale=-1.0).then_inc(e_ready, 1)
                act.wait_ge(var_ready, 1)
                A.sqrt(t_a[:, :], t_b[:, :]).then_inc(root_ready, 1)
                act.wait_ge(norm2_ready, 1)
                with act.Fori(0, NT) as T:
                    row = acc[:, bass.ds(T, 1), 0:D].rearrange("p o d -> p (o d)")
                    A.activation(row, row, ACT.Identity, bias=shift[:, bass.ds(T, 1)], scale=rstd[:, bass.ds(T, 1)]).then_inc(normed, 1)
                act.wait_ge(var_ready, 2)
                A.sqrt(t_a[:, :], t_b[:, :]).then_inc(root_ready, 1)
                act.wait_ge(norm2_ready, 2)
                with act.Fori(0, NT) as T:
                    A.activation(ks[:, bass.ds(T, 1), 1, :].rearrange("p o d -> p (o d)"), xs[:, bass.ds(T, 1), :].rearrange("p o d -> p (o d)"), ACT.Relu,
                                 bias=shift[:, bass.ds(T, 1)], scale=rstd[:, bass.ds(T, 1)]).then_inc(h2_ready, 1)

            @block.sync
            def _(sp):
                with sp.Fori(0, NG) as g:
                    sp.wait_ge(h2_ready, g * NB + NB)
                    sp.dma_start(h_tab[bass.ds(g * (NB * P), NB * P), :].rearrange("(t p) d -> p t d", p=P), ks[:, bass.ds(g * NB, NB), 1, :]).then_inc(h2_stored, 16)
                sp.wait_ge(h2_stored, 16 * NG)

            @block.gpsimd
            def _(pool):
                pool.wait_ge(normed, NT)
                pool.wait_ge(var_ready, 2)

        with nc.Block() as block:
            @block.gpsimd
            def _(pool):
                G.memset(acc[:, :, 0:D], 0.0)

        stage.close()
        h_ring = tb("h_ring", [P, U, D])
        hot = tb("hot2", [P, U, P])
        with nc.Block() as block:
            sums_done, sums_added, hot_ready = sem("n_sums_done"), sem("n_sums_added"), sem("n_hot_ready")
            got, pool_part, index_first, index_next = gather_rows("h", h_tab, lambda u: h_ring[:, u, :], lambda u: [(sums_done, U, u + 1)])

            @block.gpsimd
            def _(pool):
                pool_part(pool)

            @block.scalar
            def _(act):
                index_first(act)
                with act.Fori(0, ITERS) as i:
                    index_next(act, i)

            @block.tensor
            def _(pe):
                pe.sem_inc(sums_done, U)
                with pe.Fori(0, ITERS) as i:
                    for u in range(U):
                        if u % Q == 0:
                            pe.wait_ge(hot_ready, i * NQ + (u // Q + 1))
                        pe.wait_ge(got[u], i * 16 + 16)
                        pe.wait_ge(sums_added, i * U + (u + 1))
                        T_.matmul(bank[u % 4][:, 0:D], hot[:, u, :], h_ring[:, u, :], start=True, stop=True).then_inc(sums_done, 1)

            @block.vector
            def _(dve):
                dve.sem_inc(sums_added, 4)
                with dve.Fori(0, ITERS) as i:
                    tiles = load_node_tiles(dve, i)

                    def add(u):
                        dve.wait_ge(sums_done, i * U + (U + u + 1))
                        a = acc[:, bass.ds(tiles[u], 1), 0:D].rearrange("p o d -> p (o d)")
                        V.tensor_tensor(a, a, bank[u % 4][:, 0:D], ALU.add).then_inc(sums_added, 1)
                        dve.wait_ge(sums_added, i * U + (4 + u + 1))
                    for n in range(NQ):
                        for u in range(n * Q, (n + 1) * Q):
                            last = V.tensor_scalar(hot[:, u, :], iota_f[:, 0:P], v_loc[:, bass.ds(i * U + u, 1)], v_wgt[:, bass.ds(i * U + u, 1)],
                                                   ALU.is_equal, ALU.mult)
                        last.then_inc(hot_ready, 1)
                        if n > 0:
                            for u in range((n - 1) * Q, n * Q):
                                add(u)
                    for u in range((NQ - 1) * Q, U):
                        add(u)

        stage.close()
        h_buf = tb("mean_buf", [P, 2, D])
        hT = tb("in_T", [P, 2, 4, P])
        res = tb("res", [P, 2, D])
        with nc.Block() as block:
            mean_ready, turned, inT_ready, out_done, out_ready = [sem("f_" + n) for n in "mean turned inT out_done out_ready".split()]
            stored = [sem("f_stored0"), sem("f_stored1")]

            @block.scalar
            def _(act):
                def mean_of(T, b):
                    A.activation(h_buf[:, b, :], acc[:, bass.ds(T, 1), 0:D].rearrange("p o d -> p (o d)"), ACT.Copy,
                                 scale=rdeg[:, bass.ds(T, 1)]).then_inc(mean_ready, 1)
                    A.copy(res[:, b, :], ks[:, bass.ds(T, 1), 1, :].rearrange("p o d -> p (o d)")).then_inc(mean_ready, 1)
                act.sem_inc(inT_ready, 1)
                act.sem_inc(turned, 1)
                mean_of(0, 0)

                def body(T, i, b, last):
                    if not last:
                        act.wait_ge(turned, T + 1)
                        mean_of(T + 1, 1 - b)
                    act.wait_ge(turned, T + 2)
                    A.copy(hT[:, b, :, :].rearrange("p c n -> p (c n)"), bank[b][:, :]).then_inc(inT_ready, 1)
                pairs(act, body)

            @block.tensor
            def _(pe):
                def turn(T, b):
                    for c in range(4):
                        t = h_buf if c < 2 else res
                        last = T_.transpose(bank[b][:, c * P:(c + 1) * P], t[:, b, (c % 2) * P:(c % 2 + 1) * P], ident[:, :])
                    last.then_inc(turned, 1)
                pe.wait_ge(mean_ready, 2)
                turn(0, 0)

                def body(T, i, b, last):
                    if not last:
                        pe.wait_ge(mean_ready, T * 2 + 4)
                        pe.wait_ge(inT_ready, T + 1)
                        turn(T + 1, 1 - b)
                    pe.wait_ge(inT_ready, T + 2)
                    pe.wait_ge(out_ready, T + 1)
                    for c in range(4):
                        mm = T_.matmul(bank[2 + b][:, 0:D], hT[:, b, c, :], w1T[:, c, :], start=(c == 0), stop=(c == 3))
                    mm.then_inc(out_done, 1)
                pairs(pe, body)

            @block.vector
            def _(dve):
                chain = Chain(dve, "final_chain")
                f = chain.follow
                dve.sem_inc(out_ready, 2)
                f(V.tensor_tensor(xs[:, :, :], xs[:, :, :], b1s[:, :].unsqueeze(1).to_broadcast([P, NT, D]), ALU.add))

                def body(T, i, b, last):
                    dve.wait_ge(out_done, T + 1)
                    row = xs[:, bass.ds(T, 1), :].rearrange("p o d -> p (o d)")
                    V.tensor_tensor(row, row, bank[2 + b][:, 0:D], ALU.add).then_inc(out_ready, 1)
                pairs(dve, body)

            @block.sync
            def _(sp):
                with sp.Fori(0, NT - 1) as T:
                    sp.wait_ge(out_ready, T + 3)
                    sp.dma_start(out[bass.ds(T * P, P), :], xs[:, bass.ds(T, 1), :].rearrange("p o d -> p (o d)")).then_inc(stored[0], 16)
                sp.wait_ge(out_ready, NT + 2)
                sp.dma_start(out[(NT - 1) * P:N, :], xs[0:LAST_ROWS, NT - 1, :]).then_inc(stored[1], 16)
                sp.wait_ge(stored[0], 16 * (NT - 1))
                sp.wait_ge(stored[1], 16)
        stage.close()


_INS = ['x', 'src', 'dst', 'edge_weight1', 'L0_gnn_Wq', 'L0_gnn_bq', 'L0_gnn_Wk', 'L0_gnn_bk', 'L0_gnn_Wv', 'L0_gnn_bv',
        'L0_gnn_Wskip', 'L0_gnn_bskip', 'L0_gnn_Wgate', 'L0_gnn_bgate', 'L0_gnn_ln_w', 'L0_gnn_ln_b',
        'L0_gnn_prelu_a', 'L1_gnn_W', 'L1_gnn_b']
_OUTS = [((3125, 256), 'float32')]


def kernel(**inputs):
    import numpy as _np
    import concourse.bacc as _bacc
    from concourse import mybir as _mybir
    from concourse.bass_utils import run_bass_kernel_spmd as _run

    nc = _bacc.Bacc("TRN2", target_bir_lowering=False, num_devices=1)
    arrays, args = {}, []
    for name in _INS:
        a = _np.ascontiguousarray(inputs[name])
        if a.ndim == 0:
            a = a.reshape(1)
        arrays[f"in_{name}_dram"] = a
        args.append(nc.dram_tensor(f"in_{name}_dram", a.shape, _mybir.dt.from_np(a.dtype), kind="ExternalInput").ap())
    for i, (shape, dtype) in enumerate(_OUTS):
        dt = _mybir.dt.from_np(_np.dtype(dtype))
        args.append(nc.dram_tensor(f"out_{i}_dram", shape, dt, kind="ExternalOutput").ap())
    gnn_kernel(nc, *args)
    r = _run(nc, [arrays], core_ids=[0])
    got = tuple(r.results[0][f"out_{i}_dram"] for i in range(len(_OUTS)))
    return got[0]
```

```python
import concourse.bass as bass
from concourse import mybir
from contextlib import ExitStack

F32 = mybir.dt.float32
I32 = mybir.dt.int32
ALU = mybir.AluOpType
ACT = mybir.ActivationFunctionType
AX = mybir.AxisListType

P = 128
HEADS = 4


def gnn_kernel(nc, x, src, dst, edge_weight, Wq, bq, Wk, bk, Wv, bv, Wskip, bskip, Wgate, bgate,
               ln_w, ln_b, prelu_a, W1, b1, out):
    N, D = x.shape
    E = src.shape[0]
    DH = D // HEADS
    NT = -(-N // P)
    LAST_ROWS = N - (NT - 1) * P
    ET = -(-E // P)
    LAST_EDGES = E - (ET - 1) * P
    STEPS = ET + NT - 1
    U = 20
    ITERS = STEPS // U
    assert STEPS % U == 0
    EC = 4
    ER = ET // EC
    SC = 4
    SR = STEPS // SC
    assert ET % EC == 0 and STEPS % SC == 0 and ER <= P and SR <= P
    LAST_C = (ET - 1) // ER
    LAST_P = (ET - 1) % ER
    NB = 5
    NG = NT // NB
    assert NT % NB == 0
    SCALE = float(DH) ** -0.5
    NEG = -1.0e30
    FAR = 1 << 20
    DEN = D
    DEG = D + HEADS
    AW = D + 8

    qv_tab = nc.dram_tensor("qv_tab", (NT * P, 2 * D), F32, kind="Internal").ap()
    v_rows = nc.dram_tensor("v_rows", (STEPS, P, D), F32, kind="Internal").ap()
    h_tab = nc.dram_tensor("h_tab", (NT * P, D), F32, kind="Internal").ap()

    with ExitStack() as ctx:
        def sb(name, shape, dt=F32):
            return ctx.enter_context(nc.sbuf_tensor(name, shape, dt))

        stage = ExitStack()

        def tb(name, shape, dt=F32):
            return stage.enter_context(nc.sbuf_tensor(name, shape, dt))

        def sem(name):
            return ctx.enter_context(nc.semaphore(name))

        xs = sb("xs", [P, NT, D])
        ks = sb("ks", [P, NT, 2, D])
        w1T = sb("w1T", [P, 4, D])
        gate = sb("gate", [P, 3 * D])
        gate_u = sb("gate_u", [P, D])
        gate_w = sb("gate_w", [P, D])
        lnw = sb("lnw", [P, D])
        lnb = sb("lnb", [P, D])
        b1s = sb("b1s", [P, D])
        bg = sb("bg", [P, 1])
        pa = sb("pa", [P, 1])
        ident = sb("ident", [P, P])
        ones = sb("ones", [P, P])
        iota_f = sb("iota_f", [P, STEPS])
        t_row = sb("t_row", [P, STEPS])
        t_int = sb("t_int", [1, STEPS], I32)
        v_src = sb("v_src", [P, STEPS + U], I32)
        v_loc = sb("v_loc", [P, STEPS + U])
        v_wgt = sb("v_wgt", [P, STEPS + U])
        maskb = sb("maskb", [P, STEPS])
        row_start = sb("row_start", [SR, SC, P])
        src_stage = sb("src_stage", [P, U], I32)
        stats = sb("stats", [P, NT, 6])
        mean = sb("mean", [P, NT])
        rstd = sb("rstd", [P, NT])
        shift = sb("shift", [P, NT])
        t_a = sb("t_a", [P, NT])
        t_b = sb("t_b", [P, NT])
        pcol = sb("pcol", [P, 1])
        score = sb("score", [P, STEPS * HEADS])
        zz = sb("zz", [P, NT])
        zs = sb("zs", [P, NT])
        rden = sb("rden", [P, NT, HEADS])
        rdeg = sb("rdeg", [P, NT])

        passed, passed2 = sem("passed"), sem("passed2")

        bank = [ctx.enter_context(nc.psum_tensor(f"bank{i}", [P, 512], F32)) for i in range(8)]

        class Chain:

            def __init__(self, eng, name):
                self.eng, self.sem, self.n = eng, sem(name), 0

            def follow(self, ins):
                ins.then_inc(self.sem, 1)
                self.n = self.n + 1
                self.eng.wait_ge(self.sem, self.n)

            def pass_wait(self):
                self.eng.sem_inc(passed, 1)

            def enter(self, i, per):
                self.base, self.per = self.n, per
                self.n = i * per + self.base

            def leave(self, count):
                self.n = self.base + self.per * count

        V, A, G, T_ = nc.vector, nc.scalar, nc.gpsimd, nc.tensor

        proj = ExitStack()

        def pj(name, shape, dt=F32):
            return proj.enter_context(nc.sbuf_tensor(name, shape, dt))

        wT = pj("wT", [P, 2, 4 * D])
        bias = pj("bias", [P, 4 * D])

        wnat = tb("wnat", [P, 8, D])
        w1nat = tb("w1nat", [P, 2, 2 * D])
        iota_i = tb("iota_i", [P, STEPS], I32)
        part_i = tb("part_i", [P, EC], I32)
        part_f = tb("part_f", [P, EC])
        step_i = tb("step_i", [P, SC], I32)
        step_f = tb("step_f", [P, SC])
        bound_i = tb("bound_i", [P, NT - 1], I32)
        bound_f = tb("bound_f", [P, NT - 1])
        nt_i = tb("nt_i", [P, NT - 1], I32)
        nt_f = tb("nt_f", [P, NT - 1])
        e_int = tb("e_int", [ER, 2, EC, P], I32)
        e_src = tb("e_src", [ER, EC, P])
        e_dst = tb("e_dst", [ER, EC, P])
        e_wgt = tb("e_wgt", [ER, EC, P])
        e_start = tb("e_start", [ER, EC, P])
        prev_i = tb("prev_i", [ER, EC], I32)
        prev_f = tb("prev_f", [ER, EC])
        below = tb("below", [ER, NT - 1, EC])
        turn = tb("turn", [P, NT - 1])
        reached = tb("reached", [SR, SC, NT - 1])
        tcol = tb("tcol", [SR, SC])
        tcol_bc = tb("tcol_bc", [SR, SC, P])
        r_row = tb("r_row", [P, STEPS])
        sel = tb("sel", [ER, EC, STEPS])
        row_in = tb("row_in", [SR, SC, P])
        pcol_i = tb("pcol_i", [P, 1], I32)
        h_buf = tb("h_buf", [P, 2, D])
        hT = tb("hT", [P, 2, 2, P])
        qv_out = tb("qv_out", [P, 2, 2 * D])

        def moments(f):
            m0, v0, m1, v1 = stats[:, :, 1], stats[:, :, 2], stats[:, :, 4], stats[:, :, 5]
            V.tensor_tensor(t_a[:, :], m0, m1, ALU.subtract)
            V.tensor_tensor(mean[:, :], m0, m1, ALU.add)
            f(V.tensor_tensor(t_b[:, :], v0, v1, ALU.add))
            f(V.tensor_tensor(t_a[:, :], t_a[:, :], t_a[:, :], ALU.mult))
            V.tensor_scalar(mean[:, :], mean[:, :], 0.5, None, ALU.mult)
            V.tensor_scalar(t_a[:, :], t_a[:, :], 0.25, None, ALU.mult)
            f(V.tensor_scalar(t_b[:, :], t_b[:, :], 1.0 / D, 1e-5, ALU.mult, ALU.add))
            f(V.tensor_tensor(t_b[:, :], t_b[:, :], t_a[:, :], ALU.add))

        def pairs(eng, body, between=()):
            first = -(-len(between) // 2)
            for T in range(2 * first):
                body(T, T // 2, T % 2, False)
                if T < len(between):
                    between[T]()
            with eng.Fori(first, NT // 2) as i:
                body(i * 2, i, 0, False)
                body(i * 2 + 1, i, 1, False)
            body(NT - 1, NT // 2, 0, True)

        def nothing():
            pass

        with nc.Block() as block:
            x_zeroed, small_in, gate_in = sem("x_zeroed"), sem("small_in"), sem("gate_in")
            x_in = [sem(f"x_in{g}") for g in range(NG)]
            weights_in, w1_in, edges_in, edges_padded = sem("weights_in"), sem("w1_in"), sem("edges_in"), sem("edges_padded")
            consts_set, masks_set = sem("consts_set"), sem("masks_set")
            weightsT, below_ready, below_summed = sem("weightsT"), sem("below_ready"), sem("below_summed")
            tcol_ready, trow_summed, weights_copied = sem("tcol_ready"), sem("trow_summed"), sem("weights_copied")
            sel_ready = sem("sel_ready")
            picked, pick_read = sem("picked"), sem("pick_read")
            var_ready, root_ready, norm_ready = sem("var_ready"), sem("root_ready"), sem("norm_ready")
            h_ready, h_turned, hT_ready = sem("h_ready"), sem("h_turned"), sem("hT_ready")
            proj_done, proj_read, rows_ready = sem("proj_done"), sem("proj_read"), sem("rows_ready")
            rows_stored = [sem("rows_stored0"), sem("rows_stored1")]

            @block.sync
            def _(sp):
                for g in range(NG):
                    lo, hi = g * NB, min((g + 1) * NB, NT - 1)
                    sp.dma_start(xs[:, lo:hi, :], x[lo * P:hi * P, :].rearrange("(t p) d -> p t d", p=P)).then_inc(x_in[g], 16)
                sp.wait_ge(x_zeroed, 1)
                sp.dma_start(xs[0:LAST_ROWS, NT - 1, :], x[(NT - 1) * P:N, :]).then_inc(x_in[NG - 1], 16)
                for n, w in enumerate((Wq, Wv, Wk, Wskip)):
                    sp.dma_start(wnat[:, 2 * n:2 * n + 2, :], w.rearrange("(b p) d -> p b d", p=P)).then_inc(weights_in, 16)
                for n, vec in enumerate((bq, bv, bk, bskip)):
                    sp.dma_start(bias[:, n * D:(n + 1) * D], vec.partition_broadcast(P)).then_inc(gate_in, 16)
                sp.dma_start(gate[:, :], Wgate[0, :].partition_broadcast(P)).then_inc(gate_in, 16)
                sp.dma_start(w1nat[:, :, :], W1.rearrange("(b p) d -> p b d", p=P)).then_inc(w1_in, 16)
                sp.dma_start(lnw[:, :], ln_w.partition_broadcast(P)).then_inc(small_in, 16)
                sp.dma_start(lnb[:, :], ln_b.partition_broadcast(P)).then_inc(small_in, 16)
                sp.dma_start(b1s[:, :], b1.partition_broadcast(P)).then_inc(small_in, 16)
                sp.dma_start(bg[:, :], bgate.partition_broadcast(P)).then_inc(small_in, 16)
                sp.dma_start(pa[:, :], prelu_a.partition_broadcast(P)).then_inc(small_in, 16)

                def body(T, i, b, last):
                    sp.wait_ge(rows_ready, T + 1)
                    sp.dma_start(qv_tab[bass.ds(T * P, P), :], qv_out[:, b, :]).then_inc(rows_stored[b], 16)

                pairs(sp, body)
                sp.wait_ge(rows_stored[0], 16 * (NT // 2 + 1) + 16)
                sp.wait_ge(rows_stored[1], 16 * (NT // 2) + 16)
                sp.wait_ge(small_in, 80)

            @block.gpsimd
            def _(pool):
                G.memset(e_int[:, 0, LAST_C, :], 0).then_inc(edges_padded, 1)
                G.memset(e_int[:, 1, LAST_C, :], FAR).then_inc(edges_padded, 1)
                G.memset(e_wgt[:, LAST_C, :], 0.0).then_inc(edges_padded, 1)
                G.memset(prev_i[:, :], -1).then_inc(edges_padded, 1)
                G.memset(xs[:, NT - 1, :], 0.0).then_inc(x_zeroed, 1)
                G.memset(ident[:, :], 0.0).then_inc(masks_set, 1)
                pool.wait_ge(masks_set, 1)
                G.affine_select(out=ident[:, :], in_=ident[:, :], compare_op=ALU.not_equal, fill=1.0,
                                base=0, pattern=[[-1, P]], channel_multiplier=1).then_inc(masks_set, 1)
                G.iota(iota_i[:, :], [[1, STEPS]], base=0, channel_multiplier=0).then_inc(consts_set, 1)
                G.iota(part_i[:, :], [[ER, EC]], base=0, channel_multiplier=1).then_inc(consts_set, 1)
                G.iota(step_i[:, :], [[SR, SC]], base=0, channel_multiplier=1).then_inc(consts_set, 1)
                G.iota(bound_i[:, :], [[P, NT - 1]], base=P, channel_multiplier=0).then_inc(consts_set, 1)
                G.iota(nt_i[:, :], [[1, NT - 1]], base=1, channel_multiplier=0).then_inc(consts_set, 1)
                G.iota(pcol_i[:, :], [[0, 1]], base=0, channel_multiplier=1).then_inc(consts_set, 1)
                G.memset(ones[:, :], 1.0).then_inc(consts_set, 1)
                G.memset(v_src[:, STEPS:STEPS + U], 0)
                G.memset(v_loc[:, STEPS:STEPS + U], -1.0)
                G.memset(v_wgt[:, STEPS:STEPS + U], 0.0)

            @block.scalar
            def _(act):
                act.wait_ge(edges_padded, 4)
                full = LAST_C * ER * P
                rest = (ET - 1) * P
                for n, arr in enumerate((src, dst)):
                    act.dma_start(e_int[:, n, 0:LAST_C, :], arr[0:full].rearrange("(c r e) -> r c e", r=ER, e=P)).then_inc(edges_in, 16)
                    act.dma_start(e_int[0:LAST_P, n, LAST_C, :], arr[full:rest].rearrange("(r e) -> r e", e=P)).then_inc(edges_in, 16)
                    act.dma_start(e_int[LAST_P:LAST_P + 1, n, LAST_C, 0:LAST_EDGES], arr[rest:E].unsqueeze(0)).then_inc(edges_in, 16)
                last_of = dst[0:rest].rearrange("(k e) -> k e", e=P)[:, P - 1:P]
                act.dma_start(prev_i[1:ER, 0:1], last_of[0:ER - 1, :], allow_slow_non_contiguous=True).then_inc(edges_in, 16)
                for c in range(1, EC):
                    act.dma_start(prev_i[:, c:c + 1], last_of[c * ER - 1:(c + 1) * ER - 1, :], allow_slow_non_contiguous=True).then_inc(edges_in, 16)
                wgt = edge_weight.rearrange("e o -> (e o)")
                act.dma_start(e_wgt[:, 0:LAST_C, :], wgt[0:full].rearrange("(c r e) -> r c e", r=ER, e=P)).then_inc(edges_in, 16)
                act.dma_start(e_wgt[0:LAST_P, LAST_C, :], wgt[full:rest].rearrange("(r e) -> r e", e=P)).then_inc(edges_in, 16)
                act.dma_start(e_wgt[LAST_P:LAST_P + 1, LAST_C, 0:LAST_EDGES], wgt[rest:E].unsqueeze(0)).then_inc(edges_in, 16)
                act.wait_ge(var_ready, 1)
                A.sqrt(t_a[:, :], t_b[:, :]).then_inc(root_ready, 1)
                for c in range(2):
                    for half in range(2):
                        act.wait_ge(weightsT, 2 * c + half + 1)
                        A.copy(wT[:, c, half * 512:(half + 1) * 512], bank[2 * c + half][:, :]).then_inc(weights_copied, 1)
                act.wait_ge(norm_ready, 1)

                def copy_w1():
                    for k in range(2):
                        act.wait_ge(weightsT, 5 + k)
                        A.copy(w1T[:, 2 * k:2 * k + 2, :], bank[6 + k][:, :].rearrange("p (k d) -> p k d", k=2)).then_inc(weights_copied, 1)

                def normalise(T, b):
                    A.activation(h_buf[:, b, :], xs[:, bass.ds(T, 1), :].rearrange("p o d -> p (o d)"), ACT.Relu,
                                 bias=shift[:, bass.ds(T, 1)], scale=rstd[:, bass.ds(T, 1)]).then_inc(h_ready, 1)
                act.sem_inc(hT_ready, 1)
                act.sem_inc(h_turned, 1)
                normalise(0, 0)

                def body(T, i, b, last):
                    if not last:
                        act.wait_ge(h_turned, T + 1)
                        normalise(T + 1, 1 - b)
                    act.wait_ge(h_turned, T + 2)
                    A.copy(hT[:, b, :, :].rearrange("p c n -> p (c n)"), bank[b][:, 0:2 * P]).then_inc(hT_ready, 1)
                pairs(act, body, [nothing] * 7 + [copy_w1])

            @block.tensor
            def _(pe):
                def pick(to, what):
                    for c in range(EC):
                        last = T_.matmul(to, what[:, c, :], sel[:, c, :], start=(c == 0), stop=(c == EC - 1))
                    last.then_inc(picked, 1)

                def count_below():
                    pe.wait_ge(below_ready, 1)
                    for c in range(EC):
                        last = T_.matmul(bank[6][:, 0:NT - 1], ones[0:ER, :], below[:, :, c], start=(c == 0), stop=(c == EC - 1))
                    last.then_inc(below_summed, 1)

                def spread_t():
                    pe.wait_ge(tcol_ready, 1)
                    for c in range(SC):
                        last = T_.matmul(bank[7][:, c * SR:(c + 1) * SR], tcol_bc[:, c, :], ident[0:SR, 0:SR], start=True, stop=True)
                    last.then_inc(trow_summed, 1)

                def pick_dst():
                    pe.wait_ge(sel_ready, 1)
                    pick(bank[6][:, 0:STEPS], e_dst)

                def pick_src():
                    pick(bank[7][:, 0:STEPS], e_src)

                def pick_wgt():
                    pe.wait_ge(pick_read, 1)
                    pick(bank[6][:, 0:STEPS], e_wgt)

                def turn_locals():
                    pe.wait_ge(pick_read, 2)
                    for sc in range(SC):
                        last = T_.transpose(bank[7][0:SR, sc * P:(sc + 1) * P], v_loc[:, sc * SR:(sc + 1) * SR], ident[:, :])
                    last.then_inc(picked, 1)

                def pick_starts():
                    pe.wait_ge(pick_read, 3)
                    for sc in range(SC):
                        for c in range(EC):
                            last = T_.matmul(bank[6][0:SR, sc * P:(sc + 1) * P], sel[:, c, sc * SR:(sc + 1) * SR], e_start[:, c, :],
                                             start=(c == 0), stop=(c == EC - 1))
                    last.then_inc(picked, 1)

                def turn_w1():
                    pe.wait_ge(w1_in, 16)
                    pe.wait_ge(pick_read, 5)
                    for k2 in range(2):
                        for k in range(2):
                            for b in range(2):
                                last = T_.transpose(bank[6 + k2][:, (2 * k + b) * P:(2 * k + b + 1) * P],
                                                    w1nat[:, b, (2 * k2 + k) * P:(2 * k2 + k + 1) * P], ident[:, :])
                        last.then_inc(weightsT, 1)

                pe.wait_ge(masks_set, 2)
                pe.wait_ge(weights_in, 64)
                for c in range(2):
                    for half in range(2):
                        for b in range(4):
                            last = T_.transpose(bank[2 * c + half][:, b * P:(b + 1) * P], wnat[:, 4 * half + b, c * P:(c + 1) * P], ident[:, :])
                        last.then_inc(weightsT, 1)
                pe.wait_ge(weights_copied, 4)
                def turn_h(b):
                    for c in range(2):
                        last = T_.transpose(bank[b][:, c * P:(c + 1) * P], h_buf[:, b, c * P:(c + 1) * P], ident[:, :])
                    last.then_inc(h_turned, 1)
                pe.wait_ge(h_ready, 1)
                turn_h(0)

                def body(T, i, b, last):
                    if not last:
                        pe.wait_ge(h_ready, T + 2)
                        pe.wait_ge(hT_ready, T + 1)
                        turn_h(1 - b)
                    pe.wait_ge(hT_ready, T + 2)
                    pe.wait_ge(proj_read, T + 1)
                    for n, (lo, hi) in enumerate(((0, 2 * D), (2 * D, 3 * D))):
                        for c in range(2):
                            mm = T_.matmul(bank[2 + 2 * b + n][:, 0:hi - lo], hT[:, b, c, :], wT[:, c, lo:hi],
                                           start=(c == 0), stop=(c == 1))
                        mm.then_inc(proj_done, 1)
                pairs(pe, body, [count_below, spread_t, pick_dst, pick_src, pick_wgt, turn_locals, pick_starts, turn_w1])

            @block.vector
            def _(dve):
                chain = Chain(dve, "first_chain")
                f = chain.follow
                for T in range(NT):
                    if T % NB == 0:
                        dve.wait_ge(x_in[T // NB], 32 if T // NB == NG - 1 else 16)
                    last = V.bn_stats(stats[:, T, :], xs[:, T, :])
                f(last)
                moments(f)
                V.tensor_copy(h_buf[:, 0, 0:1], t_b[:, 0:1]).then_inc(var_ready, 1)
                dve.wait_ge(consts_set, 7)
                V.tensor_copy(iota_f[:, :], iota_i[:, :])
                V.tensor_copy(part_f[:, :], part_i[:, :])
                V.tensor_copy(step_f[:, :], step_i[:, :])
                V.tensor_copy(bound_f[:, :], bound_i[:, :])
                V.tensor_copy(pcol[:, :], pcol_i[:, :])
                f(V.tensor_copy(nt_f[:, :], nt_i[:, :]))
                dve.wait_ge(root_ready, 1)
                f(V.reciprocal(rstd[:, :], t_a[:, :]))
                V.scalar_tensor_tensor(shift[:, :], mean[:, :], -1.0, rstd[:, :], ALU.mult, ALU.mult).then_inc(norm_ready, 1)
                dve.wait_ge(edges_in, 13 * 16)
                V.tensor_copy(e_src[:, :, :], e_int[:, 0, :, :])
                V.tensor_copy(e_dst[:, :, :], e_int[:, 1, :, :])
                f(V.tensor_copy(prev_f[:, :], prev_i[:, :]))
                V.tensor_tensor(below[:, :, :], bound_f[0:ER, :].unsqueeze(2).to_broadcast([ER, NT - 1, EC]),
                                e_dst[:, :, P - 1].unsqueeze(1).to_broadcast([ER, NT - 1, EC]), ALU.is_gt).then_inc(below_ready, 1)
                V.tensor_tensor(e_start[:, :, 1:P], e_dst[:, :, 1:P], e_dst[:, :, 0:P - 1], ALU.not_equal)
                V.tensor_tensor(e_start[:, :, 0], e_dst[:, :, 0], prev_f[:, :], ALU.not_equal)
                dve.wait_ge(gate_in, 80)
                V.tensor_tensor(gate_w[:, :], gate[:, D:2 * D], gate[:, 2 * D:3 * D], ALU.subtract)
                f(V.tensor_tensor(gate_u[:, :], gate[:, 0:D], gate[:, 2 * D:3 * D], ALU.add))
                dve.sem_inc(proj_read, 2)
                dve.sem_inc(rows_stored[0], 16)
                dve.sem_inc(rows_stored[1], 16)

                def staircase():
                    dve.wait_ge(below_summed, 1)
                    f(V.tensor_tensor(turn[:, :], bank[6][:, 0:NT - 1], nt_f[:, :], ALU.add))
                    f(V.tensor_tensor(reached[:, :, :], step_f[0:SR, :].unsqueeze(2).to_broadcast([SR, SC, NT - 1]),
                                      turn[0:SR, :].unsqueeze(1).to_broadcast([SR, SC, NT - 1]), ALU.is_ge))
                    f(V.tensor_reduce(tcol[:, :], reached[:, :, :], AX.X, ALU.add))
                    V.tensor_copy(tcol_bc[:, :, :], tcol[:, :].unsqueeze(2).to_broadcast([SR, SC, P])).then_inc(tcol_ready, 1)

                def select():
                    dve.wait_ge(trow_summed, 1)
                    f(V.tensor_copy(t_row[:, :], bank[7][:, 0:STEPS]))
                    V.tensor_copy(t_int[:, :], t_row[0:1, :])
                    f(V.tensor_tensor(r_row[:, :], iota_f[:, :], t_row[:, :], ALU.subtract))
                    for c in range(EC):
                        last = V.tensor_scalar(sel[:, c, :], r_row[0:ER, :], part_f[0:ER, c:c + 1], None, ALU.is_equal)
                    last.then_inc(sel_ready, 1)

                def read_dst():
                    dve.wait_ge(picked, 1)
                    f(V.scalar_tensor_tensor(v_loc[:, 0:STEPS], t_row[:, :], float(-P), bank[6][:, 0:STEPS], ALU.mult, ALU.add))
                    f(V.tensor_scalar(v_loc[:, 0:STEPS], v_loc[:, 0:STEPS], -1.0, float(P), ALU.max, ALU.min))
                    V.tensor_scalar(r_row[:, :], v_loc[:, 0:STEPS], 0.0, NEG, ALU.is_lt, ALU.mult)
                    f(V.tensor_scalar(maskb[:, :], v_loc[:, 0:STEPS], float(P), NEG, ALU.is_ge, ALU.mult))
                    V.tensor_tensor(maskb[:, :], maskb[:, :], r_row[:, :], ALU.add).then_inc(pick_read, 1)

                def read_src():
                    dve.wait_ge(picked, 2)
                    V.tensor_copy(v_src[:, 0:STEPS], bank[7][:, 0:STEPS]).then_inc(pick_read, 1)

                def read_wgt():
                    dve.wait_ge(picked, 3)
                    V.tensor_copy(v_wgt[:, 0:STEPS], bank[6][:, 0:STEPS]).then_inc(pick_read, 1)

                def read_locals():
                    dve.wait_ge(picked, 4)
                    locals_v = bank[7][0:SR, :].rearrange("p (c e) -> p c e", c=SC)
                    V.tensor_scalar(row_in[:, :, :], locals_v, 0.0, NEG, ALU.is_ge, ALU.mult)
                    f(V.tensor_scalar(row_start[:, :, :], locals_v, float(P), None, ALU.is_lt))
                    V.tensor_tensor(row_in[:, :, :], row_in[:, :, :], row_start[:, :, :], ALU.mult).then_inc(pick_read, 1)

                def read_starts():
                    dve.wait_ge(pick_read, 4)
                    dve.wait_ge(picked, 5)
                    V.tensor_tensor(row_start[:, :, :], row_in[:, :, :],
                                    bank[6][0:SR, :].rearrange("p (c e) -> p c e", c=SC), ALU.mult).then_inc(pick_read, 1)

                def body(T, i, b, last):
                    dve.wait_ge(proj_done, T * 2 + 1)
                    dve.wait_ge(rows_stored[b], i * 16 + 16)
                    V.tensor_tensor(qv_out[:, b, :], bank[2 + 2 * b][:, :], bias[:, 0:2 * D], ALU.add).then_inc(rows_ready, 1)
                    dve.wait_ge(proj_done, T * 2 + 2)
                    V.tensor_tensor(ks[:, bass.ds(T, 1), 0, :].rearrange("p o d -> p (o d)"), bank[3 + 2 * b][:, 0:D],
                                    bias[:, 2 * D:3 * D], ALU.add).then_inc(proj_read, 1)
                pairs(dve, body, [staircase, select, nothing, read_dst, read_src, read_wgt, read_locals, read_starts])

        def gather_rows(tag, table, ring, slots_free):
            got = [sem(f"{tag}_got{u}") for u in range(U)]
            index_ready, claimed = sem(f"{tag}_index_ready"), sem(f"{tag}_claimed")
            H = U // 2

            def pool_part(pool):
                with pool.Fori(0, ITERS) as i:
                    for u in range(U):
                        if u % H == 0:
                            pool.wait_ge(index_ready, i * 2 + (1 + u // H))
                            pool.sem_inc(claimed, 1)
                        for signal, per, level in slots_free(u):
                            pool.wait_ge(signal, i * per + level)
                            pool.sem_inc(claimed, 1)
                        pool.indirect_dma_start(ring(u), None, table,
                                                bass.IndirectOffsetOnAxis(ap=src_stage[:, u:u + 1], axis=0)).then_inc(got[u], 16)

            def index_first(act):
                for half in range(2):
                    A.copy(src_stage[:, half * H:(half + 1) * H], v_src[:, half * H:(half + 1) * H]).then_inc(index_ready, 1)

            def index_next(act, i, between=lambda: None):
                for half in range(2):
                    if half == 1:
                        between()
                    for u in range(H):
                        act.wait_ge(got[half * H + u], i * 16 + 16)
                    A.copy(src_stage[:, half * H:(half + 1) * H], v_src[:, bass.ds(i * U + (U + half * H), H)]).then_inc(index_ready, 1)
            return got, pool_part, index_first, index_next

        def load_node_tiles(eng, i):
            _, vals = nc.values_load_multi_w_load_instructions(t_int[0:1, bass.ds(i * U, U)], engines=[eng.engine],
                                                               min_val=0, max_val=NT - 1, skip_runtime_bounds_check_because='T(t) is clamped by its construction')
            return vals

        stage.close()
        H = U // 2
        Q = 4
        qv_ring = tb("qv_ring", [P, U, 2 * D])
        hot = tb("hot1", [P, U, P])
        hotT = tb("hotT", [P, U, P])
        prod = tb("prod", [P, H, D])
        h_one = tb("h_one", [P, D])
        h_oneT = tb("h_oneT", [P, 2, P])
        dot = tb("dot1", [P, D])
        LEFT = NT - ITERS
        assert LEFT >= 0 and H // 2 <= 5
        NQ = U // Q
        assert H % 2 == 0 and U % Q == 0 and Q == 4 and NQ >= 4
        with nc.Block() as block:
            skip_h, skip_turned, skip_copied, skip_done, skip_read = [sem("skip_" + n) for n in "h turned copied done read".split()]
            hot_built, hot_turned, hotT_ready = sem("hot_built"), sem("hot_turned"), sem("hotT_ready")
            k_spread, qk_used = sem("k_spread"), sem("qk_used")
            v_stored = [sem(f"v_stored{n}") for n in range(U // Q)]
            got, pool_part, index_first, index_next = gather_rows(
                "qv", qv_tab, lambda u: qv_ring[:, u, :],
                lambda u: [(qk_used, H, u // 2 + 1)] * (u % 2 == 0) + [(v_stored[u // Q], 16, 16)] * (u % Q == 0))

            @block.gpsimd
            def _(pool):
                for n in range(U // Q):
                    pool.sem_inc(v_stored[n], 16)
                pool_part(pool)

            @block.scalar
            def _(act):
                def normalise_one(T, k):
                    act.wait_ge(skip_turned, k + 1)
                    act.sem_inc(passed2, 1)
                    A.activation(h_one[:, :], xs[:, bass.ds(T, 1), :].rearrange("p o d -> p (o d)"), ACT.Relu,
                                 bias=shift[:, bass.ds(T, 1)], scale=rstd[:, bass.ds(T, 1)]).then_inc(skip_h, 1)

                def copy_one(k):
                    act.wait_ge(skip_turned, k + 2)
                    A.copy(h_oneT[:, :, :].rearrange("p c n -> p (c n)"), bank[5][:, 0:2 * P]).then_inc(skip_copied, 1)

                def copy_hot(i, n):
                    act.wait_ge(hot_turned, i * NQ + (n + 1))
                    A.copy(hotT[:, n * Q:(n + 1) * Q, :].rearrange("p u e -> p (u e)"), bank[7][:, :]).then_inc(hotT_ready, 1)

                def second_half(i):
                    copy_one(i + LEFT)
                    copy_hot(i, NQ - 1)
                    copy_hot(i + 1, 0)
                index_first(act)
                act.sem_inc(skip_turned, 1)
                for k in range(LEFT):
                    normalise_one(ITERS + k, k)
                    copy_one(k)
                copy_hot(0, 0)
                with act.Fori(0, ITERS) as i:
                    normalise_one(i, i + LEFT)
                    for n in range(1, NQ - 1):
                        copy_hot(i, n)
                    index_next(act, i, lambda: second_half(i))

            @block.sync
            def _(sp):
                with sp.Fori(0, ITERS) as i:
                    for n in range(U // Q):
                        for u in range(n * Q, (n + 1) * Q):
                            sp.wait_ge(got[u], i * 16 + 16)
                        sp.dma_start(v_rows[bass.ds(i * U + n * Q, Q), :, :].rearrange("t p d -> p t d"), qv_ring[:, n * Q:(n + 1) * Q, D:2 * D]).then_inc(v_stored[n], 16)
                for n in range(U // Q):
                    sp.wait_ge(v_stored[n], 16 * (ITERS + 1))

            @block.tensor
            def _(pe):
                def turn_one(k):
                    pe.wait_ge(skip_h, k + 1)
                    for c in range(2):
                        last = T_.transpose(bank[5][:, c * P:(c + 1) * P], h_one[:, c * P:(c + 1) * P], ident[:, :])
                    last.then_inc(skip_turned, 1)

                def multiply_one(k):
                    pe.wait_ge(skip_copied, k + 1)
                    pe.wait_ge(skip_read, k + 1)
                    for c in range(2):
                        last = T_.matmul(bank[6][:, 0:D], h_oneT[:, c, :], wT[:, c, 3 * D:4 * D], start=(c == 0), stop=(c == 1))
                    last.then_inc(skip_done, 1)
                for k in range(LEFT):
                    turn_one(k)
                    multiply_one(k)

                def turn_hot(i, n):
                    pe.wait_ge(hot_built, i * NQ + (n + 1))
                    pe.wait_ge(hotT_ready, i * NQ + (n + 1))
                    for u in range(Q):
                        last = T_.transpose(bank[7][:, u * P:(u + 1) * P], hot[:, n * Q + u, :], ident[:, :])
                    last.then_inc(hot_turned, 1)
                pe.sem_inc(hotT_ready, 1)
                turn_hot(0, 0)
                with pe.Fori(0, ITERS) as i:
                    tiles = load_node_tiles(pe, i)
                    for n in range(NQ):
                        if n + 1 < NQ:
                            turn_hot(i, n + 1)
                        else:
                            turn_hot(i + 1, 0)
                        pe.wait_ge(hotT_ready, i * NQ + (n + 2))
                        for m in (2 * n, 2 * n + 1):
                            pe.wait_ge(qk_used, i * H + (m + 6))
                            for u in (2 * m, 2 * m + 1):
                                mm = T_.matmul(bank[m % 5][:, (u % 2) * D:(u % 2 + 1) * D], hotT[:, u, :],
                                               ks[:, bass.ds(tiles[u], 1), 0, :], start=True, stop=True)
                            mm.then_inc(k_spread, 1)
                        if n == 2:
                            turn_one(i + LEFT)
                    multiply_one(i + LEFT)

            @block.vector
            def _(dve):
                dve.sem_inc(qk_used, H)
                dve.sem_inc(skip_read, 1)

                def read_skip(T, k):
                    dve.wait_ge(skip_done, k + 1)
                    row = ks[:, bass.ds(T, 1), 1, :].rearrange("p o d -> p (o d)")
                    V.tensor_tensor(row, bank[6][:, 0:D], bias[:, 3 * D:4 * D], ALU.add).then_inc(skip_read, 1)
                    dve.wait_ge(skip_read, k + 2)
                    V.scalar_tensor_tensor(dot[:, :], row, 1.0, gate_u[:, :], ALU.mult, ALU.mult, accum_out=zs[:, bass.ds(T, 1)])

                def build(n, first):
                    V.tensor_tensor(hot[:, n * Q:(n + 1) * Q, :], iota_f[:, 0:P].unsqueeze(1).to_broadcast([P, Q, P]),
                                    v_loc[:, first].unsqueeze(2).to_broadcast([P, Q, P]), ALU.is_equal).then_inc(hot_built, 1)
                summed = sem("summed")
                build(0, slice(0, Q))
                build(1, slice(Q, 2 * Q))
                for k in range(LEFT):
                    read_skip(ITERS + k, k)
                with dve.Fori(0, ITERS) as i:
                    for m in range(H):
                        if m % 2 == 0:
                            build((m // 2 + 2) % NQ, bass.ds(i * U + (m // 2 + 2) * Q, Q))
                        dve.wait_ge(k_spread, i * H + (m + 1))
                        dve.wait_ge(got[2 * m], i * 16 + 16)
                        dve.wait_ge(got[2 * m + 1], i * 16 + 16)
                        j = m % (H // 2)
                        V.tensor_tensor(prod[:, 2 * j:2 * j + 2, :], qv_ring[:, 2 * m:2 * m + 2, 0:D],
                                        bank[m % 5][:, :].rearrange("p (u d) -> p u d", u=2), ALU.mult).then_inc(qk_used, 1)
                        if j == H // 2 - 1:
                            half = m // (H // 2)
                            dve.wait_ge(qk_used, i * H + (H + m + 1))
                            V.tensor_reduce(score[:, bass.ds(i * (U * HEADS) + half * H * HEADS, H * HEADS)],
                                            prod[:, :, :].rearrange("p u (h d) -> p (u h) d", h=HEADS), AX.X, ALU.add).then_inc(summed, 1)
                            dve.wait_ge(summed, i * 2 + (1 + half))
                    read_skip(i, i + LEFT)

        stage.close()
        proj.close()
        acc = sb("acc", [P, NT, AW])
        acc_odd = sb("acc_odd", [P, NT, AW])
        seg = tb("seg", [SR, SC, HEADS, P])
        seg2 = tb("seg2", [SR, SC, HEADS, P])
        cuts = tb("cuts", [SR, SC, HEADS, P])
        cuts_back = tb("cuts_back", [SR, SC, HEADS, P])
        next_start = tb("next_start", [SR, SC, P])
        reach = tb("reach", [SR, SC, P])
        reach_back = tb("reach_back", [SR, SC, P])
        cut_all = tb("cut_all", [SR, SC])
        ends = tb("ends", [SR, SC, 2, HEADS])
        firsts = tb("firsts", [SR, SC, HEADS])
        head_cuts = tb("head_cuts", [HEADS, STEPS])
        head_first = tb("head_first", [HEADS, STEPS])
        carry = tb("carry", [HEADS, STEPS + 1])
        carry_col = tb("carry_col", [SR, SC, HEADS])

        with nc.Block() as block:
            cuts_set, cuts_back_set = sem("cuts_set"), sem("cuts_back_set")
            masked, rows_turned, rows_copied = sem("masked"), sem("rows_turned"), sem("rows_copied")
            ends_ready, ends_turned, carry_ready, carry_turned = sem("ends_ready"), sem("ends_turned"), sem("carry_ready"), sem("carry_turned")
            max_ready, max_turned, shifted = sem("max_ready"), sem("max_turned"), sem("shifted")
            by_step = score[:, :].rearrange("p (t h) -> p t h", h=HEADS)

            @block.gpsimd
            def _(pool):
                G.memset(cuts[:, :, :, 0], NEG).then_inc(cuts_set, 1)
                G.memset(cuts_back[:, :, :, P - 1], NEG).then_inc(cuts_set, 1)
                G.memset(next_start[:, :, P - 1], 0.0).then_inc(cuts_set, 1)
                G.memset(acc[:, :, :], 0.0)
                G.memset(acc_odd[:, :, :], 0.0)

            @block.tensor
            def _(pe):
                pe.wait_ge(masked, 1)
                for sc in range(SC):
                    for h in range(HEADS):
                        last = T_.transpose(bank[sc][0:SR, h * P:(h + 1) * P], by_step[:, sc * SR:(sc + 1) * SR, h], ident[:, :])
                    last.then_inc(rows_turned, 1)
                pe.wait_ge(ends_ready, 1)
                for sc in range(SC):
                    T_.transpose(bank[7][0:HEADS, sc * SR:(sc + 1) * SR], firsts[:, sc, :], ident[0:SR, 0:SR])
                for way in range(2):
                    pe.wait_ge(ends_ready, way + 1)
                    for sc in range(SC):
                        T_.transpose(bank[4][0:HEADS, sc * SR:(sc + 1) * SR], ends[:, sc, 0, :], ident[0:SR, 0:SR])
                        last = T_.transpose(bank[5][0:HEADS, sc * SR:(sc + 1) * SR], ends[:, sc, 1, :], ident[0:SR, 0:SR])
                    last.then_inc(ends_turned, 1)
                    pe.wait_ge(carry_ready, way + 1)
                    for sc in range(SC):
                        last = T_.transpose(bank[6][0:SR, sc * HEADS:(sc + 1) * HEADS], (carry, head_cuts)[way][:, sc * SR:(sc + 1) * SR],
                                            ident[0:HEADS, 0:HEADS])
                    last.then_inc(carry_turned, 1)
                for h in range(HEADS):
                    for sc in range(SC):
                        if h == 0:
                            pe.wait_ge(max_ready, sc + 1)
                        last = T_.transpose(bank[h][:, sc * SR:(sc + 1) * SR], seg[:, sc, h, :], ident[0:SR, 0:SR])
                    last.then_inc(max_turned, 1)

            @block.scalar
            def _(act):
                A.copy(cuts[:, :, :, 1:P], row_start[:, :, 1:P].unsqueeze(2).to_broadcast([SR, SC, HEADS, P - 1])).then_inc(cuts_set, 1)
                A.copy(next_start[:, :, 0:P - 1], row_start[:, :, 1:P]).then_inc(cuts_set, 1)
                for sc in range(SC):
                    act.wait_ge(rows_turned, sc + 1)
                    A.copy(seg[:, sc, :, :].rearrange("p h e -> p (h e)"), bank[sc][0:SR, :]).then_inc(rows_copied, 1)
                A.copy(cuts_back[:, :, :, 0:P - 1], row_start[:, :, 1:P].unsqueeze(2).to_broadcast([SR, SC, HEADS, P - 1])).then_inc(cuts_back_set, 1)
                act.wait_ge(shifted, HEADS)
                A.activation(score[:, :], score[:, :], ACT.Exp, scale=SCALE)

            @block.vector
            def _(dve):
                chain = Chain(dve, "max_chain")
                f = chain.follow

                def rows(t, sc):
                    return t[:, sc, :, :].rearrange("p h e -> p (h e)")

                V.tensor_tensor(by_step, by_step, maskb[:, :].unsqueeze(2).to_broadcast([P, STEPS, HEADS]), ALU.add).then_inc(masked, 1)
                dve.wait_ge(cuts_set, 5)
                for sc in range(SC):
                    V.tensor_tensor_scan(reach[:, sc, :], row_start[:, sc, :], row_start[:, sc, :], 0.0, ALU.min, ALU.min)
                    V.tensor_tensor_scan(reach_back[:, sc, ::-1], next_start[:, sc, ::-1], next_start[:, sc, ::-1], 0.0, ALU.min, ALU.min)
                V.tensor_reduce(cut_all[:, :], row_start[:, :, :], AX.X, ALU.min)
                for sc in range(SC):
                    dve.wait_ge(rows_copied, sc + 1)
                    V.tensor_tensor_scan(rows(seg2, sc), rows(cuts, sc), rows(seg, sc), NEG, ALU.add, ALU.max)
                f(V.tensor_copy(firsts[:, :, :], row_start[:, :, 0].unsqueeze(2).to_broadcast([SR, SC, HEADS])))
                V.tensor_copy(ends[:, :, 0, :], seg2[:, :, :, P - 1])
                V.tensor_copy(ends[:, :, 1, :], cut_all[:, :].unsqueeze(2).to_broadcast([SR, SC, HEADS])).then_inc(ends_ready, 1)
                dve.wait_ge(ends_turned, 1)
                V.tensor_copy(head_first[:, :], bank[7][0:HEADS, 0:STEPS])
                V.memset(carry[:, :], NEG)
                f(V.tensor_copy(head_cuts[:, :], bank[5][0:HEADS, 0:STEPS]))
                V.tensor_tensor_scan(carry[:, 1:STEPS + 1], head_cuts[:, :], bank[4][0:HEADS, 0:STEPS], NEG, ALU.add, ALU.max).then_inc(carry_ready, 1)
                dve.wait_ge(carry_turned, 1)
                f(V.tensor_copy(carry_col[:, :, :], bank[6][0:SR, 0:SC * HEADS].rearrange("p (c h) -> p c h", c=SC)))
                for sc in range(SC):
                    for h in range(HEADS):
                        last = V.scalar_tensor_tensor(seg2[:, sc, h, :], reach[:, sc, :], carry_col[:, sc, h:h + 1], seg2[:, sc, h, :], ALU.add, ALU.max)
                f(last)
                dve.wait_ge(cuts_back_set, 1)
                for sc in range(SC):
                    last = V.tensor_tensor_scan(rows(seg, sc)[:, ::-1], rows(cuts_back, sc)[:, ::-1], rows(seg2, sc)[:, ::-1], NEG, ALU.add, ALU.max)
                f(last)
                f(V.tensor_copy(ends[:, :, 0, :], seg[:, :, :, 0]))
                V.tensor_copy(ends[:, :, 1, :], reach_back[:, :, 0].unsqueeze(2).to_broadcast([SR, SC, HEADS])).then_inc(ends_ready, 1)
                dve.wait_ge(ends_turned, 2)
                V.memset(head_cuts[:, STEPS - 1:STEPS], NEG)
                f(V.tensor_tensor(head_cuts[:, 0:STEPS - 1], bank[5][0:HEADS, 0:STEPS - 1], head_first[:, 1:STEPS], ALU.add))
                f(V.tensor_tensor_scan(carry[:, 0:STEPS][:, ::-1], head_cuts[:, ::-1], bank[4][0:HEADS, 0:STEPS][:, ::-1], NEG, ALU.add, ALU.max))
                V.tensor_tensor(head_cuts[:, 0:STEPS - 1], carry[:, 1:STEPS], head_first[:, 1:STEPS], ALU.add).then_inc(carry_ready, 1)
                dve.wait_ge(carry_turned, 2)
                f(V.tensor_copy(carry_col[:, :, :], bank[6][0:SR, 0:SC * HEADS].rearrange("p (c h) -> p c h", c=SC)))
                for sc in range(SC):
                    for h in range(HEADS):
                        last = V.scalar_tensor_tensor(seg[:, sc, h, :], reach_back[:, sc, :], carry_col[:, sc, h:h + 1], seg[:, sc, h, :], ALU.add, ALU.max)
                    last.then_inc(max_ready, 1)
                for h in range(HEADS):
                    dve.wait_ge(max_turned, h + 1)
                    V.tensor_tensor(by_step[:, :, h], by_step[:, :, h], bank[h][:, 0:STEPS], ALU.subtract).then_inc(shifted, 1)

        stage.close()
        NQ = U // Q
        ring = tb("ring", [P, U, AW])
        hot = tb("hot", [P, U, P])
        with nc.Block() as block:
            sums_done, sums_added, hot_ready, ex_ready = sem("sums_done"), sem("sums_added"), sem("hot_ready"), sem("ex_ready")
            by_act_done, by_pool_done, ones_set = sem("by_act_done"), sem("by_pool_done"), sem("ones_set")
            v_in = [sem(f"v_in{n}") for n in range(NQ)]

            @block.sync
            def _(sp):
                with sp.Fori(0, ITERS) as i:
                    for n in range(NQ):
                        sp.wait_ge(sums_done, i * U + (n + 1) * Q)
                        sp.dma_start(ring[:, n * Q:(n + 1) * Q, 0:D], v_rows[bass.ds(i * U + n * Q, Q), :, :].rearrange("t p d -> p t d")).then_inc(v_in[n], 16)

            @block.gpsimd
            def _(pool):
                G.memset(ring[:, :, D:AW], 1.0).then_inc(ones_set, 1)
                with pool.Fori(0, ITERS) as i:
                    for n in range(NQ):
                        pool.wait_ge(v_in[n], i * 16 + 16)
                        pool.sem_inc(passed, 1)
                        u = n * Q + 2
                        r = ring[:, u:u + 2, 0:D].rearrange("p u (h d) -> p u h d", h=HEADS)
                        G.tensor_tensor(r, r, score[:, bass.ds(i * (U * HEADS) + u * HEADS, 2 * HEADS)].rearrange("p (u h) -> p u h", u=2)
                                        .unsqueeze(3).to_broadcast([P, 2, HEADS, DH]), ALU.mult).then_inc(by_pool_done, 1)

            @block.scalar
            def _(act):
                act.wait_ge(ones_set, 1)
                with act.Fori(0, ITERS) as i:
                    for n in range(NQ):
                        act.wait_ge(v_in[n], i * 16 + 16)
                        act.sem_inc(passed2, 1)
                        A.copy(ring[:, n * Q:(n + 1) * Q, DEN:DEN + HEADS], score[:, bass.ds(i * (U * HEADS) + n * Q * HEADS, Q * HEADS)].rearrange("p (u h) -> p u h", u=Q)).then_inc(ex_ready, 1)
                        for u in (n * Q, n * Q + 1):
                            for h in range(HEADS):
                                part = ring[:, u, h * DH:(h + 1) * DH]
                                last = A.activation(part, part, ACT.Copy, scale=score[:, bass.ds(i * (U * HEADS) + u * HEADS + h, 1)])
                            last.then_inc(by_act_done, 1)

            @block.tensor
            def _(pe):
                pe.sem_inc(sums_done, U)
                with pe.Fori(0, ITERS) as i:
                    for u in range(U):
                        if u % Q == 0:
                            pe.wait_ge(ex_ready, i * NQ + (u // Q + 1))
                            pe.wait_ge(hot_ready, i * NQ + (u // Q + 1))
                        if u % Q < 2:
                            pe.wait_ge(by_act_done, i * (2 * NQ) + (u // Q * 2 + u % Q + 1))
                        elif u % Q == 2:
                            pe.wait_ge(by_pool_done, i * NQ + (u // Q + 1))
                        pe.wait_ge(sums_added, i * U + (u + 1))
                        T_.matmul(bank[u % 4][:, 0:DEG + 1], hot[:, u, :], ring[:, u, 0:DEG + 1], start=True, stop=True).then_inc(sums_done, 1)

            @block.vector
            def _(dve):
                dve.sem_inc(sums_added, 4)

                def build(n, first):
                    V.tensor_tensor(hot[:, n * Q:(n + 1) * Q, :], iota_f[:, 0:P].unsqueeze(1).to_broadcast([P, Q, P]),
                                    v_loc[:, first].unsqueeze(2).to_broadcast([P, Q, P]), ALU.is_equal).then_inc(hot_ready, 1)
                build(0, slice(0, Q))
                with dve.Fori(0, ITERS) as i:
                    for n in range(NQ):
                        if n < NQ - 1:
                            build(n + 1, bass.ds(i * U + (n + 1) * Q, Q))
                        else:
                            build(0, bass.ds(i * U + U, Q))
                        if n == 0:
                            tiles = load_node_tiles(dve, i)
                        for u in range(n * Q, (n + 1) * Q):
                            dve.wait_ge(sums_done, i * U + (U + u + 1))
                            dve.wait_ge(sums_added, i * U + (4 + u - 1))
                            a = (acc, acc_odd)[u % 2][:, bass.ds(tiles[u], 1), 0:DEG + 1].rearrange("p o d -> p (o d)")
                            V.tensor_tensor(a, a, bank[u % 4][:, 0:DEG + 1], ALU.add).then_inc(sums_added, 1)

        stage.close()
        dot = tb("dot2", [P, NB, D])
        one_less = tb("one_less", [P, 1])
        zc = tb("zc", [P, NT])
        BY_ACT = 3
        with nc.Block() as block:
            z_ready, e_ready, var_ready, root_ready = [sem("mid_" + n) for n in "z e var root".split()]
            counts_added, added, sums_reset = sem("counts_added"), sem("added"), sem("sums_reset")
            gate_ready, faded = sem("gate_ready"), sem("faded")
            norm2_ready, normed, scaled, shifted2, relu_ready, finished = [sem("mid_" + n) for n in "norm2 normed scaled shifted relu finished".split()]
            h2_ready, h2_dve, h2_max, h2_stored = sem("h2_ready"), sem("h2_dve"), sem("h2_max"), sem("h2_stored")

            def grp(t, g, lo=0, n=D):
                return t[:, bass.ds(g * NB, NB), lo:lo + n]

            def tile_of(t, T):
                return t[:, bass.ds(T, 1), 0:D].rearrange("p o d -> p (o d)")

            def skip_of(T):
                return ks[:, bass.ds(T, 1), 1, :].rearrange("p o d -> p (o d)")

            @block.gpsimd
            def _(pool):
                G.tensor_tensor(acc[:, :, D:AW], acc[:, :, D:AW], acc_odd[:, :, D:AW], ALU.add).then_inc(counts_added, 1)
                with pool.Fori(0, NG) as g:
                    G.tensor_tensor(grp(acc, g), grp(acc, g), grp(acc_odd, g), ALU.add).then_inc(added, 1)
                pool.wait_ge(added, NG)
                G.memset(acc_odd[:, :, 0:D], 0.0).then_inc(sums_reset, 1)
                with pool.Fori(0, NG) as g:
                    pool.wait_ge(scaled, g + 1)
                    G.tensor_tensor(grp(acc, g), grp(acc, g), lnb[:, :].unsqueeze(1).to_broadcast([P, NB, D]), ALU.add).then_inc(shifted2, 1)

            @block.vector
            def _(dve):
                chain = Chain(dve, "between_chain")
                f = chain.follow
                dve.wait_ge(counts_added, 1)
                V.tensor_scalar(one_less[:, :], pa[:, :], -1.0, 1.0, ALU.mult, ALU.add)
                V.tensor_scalar(rdeg[:, :], acc[:, :, DEG], 1.0, None, ALU.max)
                f(V.tensor_scalar(rden[:, :, :], acc[:, :, DEN:DEN + HEADS], 1e-30, None, ALU.max))
                V.reciprocal(rdeg[:, :], rdeg[:, :])
                f(V.reciprocal(rden[:, :, :], rden[:, :, :]))
                with dve.Fori(0, NG) as g:
                    chain.enter(g, 1)
                    dve.wait_ge(added, g + 1)
                    mean_v = grp(acc, g)
                    f(V.tensor_tensor(mean_v.rearrange("p t (h d) -> p t h d", h=HEADS), mean_v.rearrange("p t (h d) -> p t h d", h=HEADS),
                                      rden[:, bass.ds(g * NB, NB), :].unsqueeze(3).to_broadcast([P, NB, HEADS, DH]), ALU.mult))
                    for n in range(NB):
                        V.scalar_tensor_tensor(dot[:, n, :], tile_of(acc, g * NB + n), 1.0, gate_w[:, :], ALU.mult, ALU.mult,
                                               accum_out=zz[:, bass.ds(g * NB + n, 1)])
                chain.leave(NG)
                f(V.tensor_copy(t_a[:, 0:1], one_less[:, :]))
                f(V.tensor_tensor(zz[:, :], zz[:, :], zs[:, :], ALU.add))
                V.tensor_scalar(zz[:, :], zz[:, :], bg[:, 0:1], None, ALU.add).then_inc(z_ready, 1)
                dve.wait_ge(e_ready, 1)
                f(V.tensor_scalar(zz[:, :], zz[:, :], 1.0, None, ALU.add))
                f(V.reciprocal(zz[:, :], zz[:, :]))
                V.tensor_scalar(zc[:, :], zz[:, :], -1.0, 1.0, ALU.mult, ALU.add).then_inc(gate_ready, 1)
                with dve.Fori(0, NG) as g:
                    chain.enter(g, 1)
                    dve.wait_ge(faded, g * NB + NB)
                    for n in range(NB):
                        last = V.scalar_tensor_tensor(tile_of(acc, g * NB + n), skip_of(g * NB + n), zz[:, bass.ds(g * NB + n, 1)],
                                                      tile_of(acc, g * NB + n), ALU.mult, ALU.add)
                    f(last)
                    chain.pass_wait()
                    for n in range(NB):
                        last = V.bn_stats(stats[:, bass.ds(g * NB + n, 1), :], acc[:, bass.ds(g * NB + n, 1), 0:D])
                chain.leave(NG)
                f(V.tensor_copy(dot[:, 0, 0:1], dot[:, 0, 0:1]))
                moments(f)
                V.tensor_copy(dot[:, 0, 0:1], dot[:, 0, 0:1]).then_inc(var_ready, 1)
                dve.wait_ge(root_ready, 1)
                f(V.reciprocal(rstd[:, :], t_a[:, :]))
                V.scalar_tensor_tensor(shift[:, :], mean[:, :], -1.0, rstd[:, :], ALU.mult, ALU.mult).then_inc(norm2_ready, 1)

                def scale_rows(g):
                    dve.wait_ge(normed, g * NB + NB)
                    V.tensor_tensor(grp(acc, g), grp(acc, g), lnw[:, :].unsqueeze(1).to_broadcast([P, NB, D]), ALU.mult).then_inc(scaled, 1)

                def finish(g, ahead):
                    dve.wait_ge(shifted2, g + 1)
                    f(V.scalar_tensor_tensor(grp(xs, g), grp(acc, g), pa[:, 0:1], grp(xs, g), ALU.mult, ALU.add))
                    dve.wait_ge(relu_ready, g + 1)
                    V.scalar_tensor_tensor(grp(xs, g), ks[:, bass.ds(g * NB, NB), 1, :], one_less[:, 0:1], grp(xs, g), ALU.mult, ALU.add).then_inc(finished, 1)
                    ahead()
                    dve.wait_ge(finished, g + 1)
                    chain.pass_wait()
                    for n in range(NB):
                        V.bn_stats(stats[:, bass.ds(g * NB + n, 1), :], xs[:, bass.ds(g * NB + n, 1), :])
                scale_rows(0)
                scale_rows(1)
                with dve.Fori(0, NG - 2) as g:
                    chain.enter(g, 1)
                    finish(g, lambda: scale_rows(g + 2))
                chain.leave(NG - 2)
                finish(NG - 2, lambda: None)
                finish(NG - 1, lambda: None)
                f(V.tensor_copy(dot[:, 0, 0:1], dot[:, 0, 0:1]))
                moments(f)
                V.tensor_copy(dot[:, 0, 0:1], dot[:, 0, 0:1]).then_inc(var_ready, 1)
                dve.wait_ge(root_ready, 2)
                f(V.reciprocal(rstd[:, :], t_a[:, :]))
                f(V.scalar_tensor_tensor(shift[:, :], mean[:, :], -1.0, rstd[:, :], ALU.mult, ALU.mult))
                V.tensor_copy(dot[:, 0, 0:1], dot[:, 0, 0:1]).then_inc(norm2_ready, 1)
                with dve.Fori(BY_ACT, NG) as g:
                    for n in range(NB):
                        T = g * NB + n
                        last = V.tensor_scalar(skip_of(T), tile_of(xs, T), rstd[:, bass.ds(T, 1)], shift[:, bass.ds(T, 1)], ALU.mult, ALU.add)
                    last.then_inc(h2_dve, 1)
                    dve.wait_ge(h2_dve, g - (BY_ACT - 1))
                    V.tensor_scalar(ks[:, bass.ds(g * NB, NB), 1, :], ks[:, bass.ds(g * NB, NB), 1, :], 0.0, None, ALU.max).then_inc(h2_max, 1)

            @block.scalar
            def _(act):
                act.wait_ge(z_ready, 1)
                A.activation(zz[:, :], zz[:, :], ACT.Exp, scale=-1.0).then_inc(e_ready, 1)
                act.wait_ge(gate_ready, 1)
                with act.Fori(0, NT) as T:
                    A.activation(tile_of(acc, T), tile_of(acc, T), ACT.Copy, scale=zc[:, bass.ds(T, 1)]).then_inc(faded, 1)
                act.wait_ge(var_ready, 1)
                A.sqrt(t_a[:, :], t_b[:, :]).then_inc(root_ready, 1)
                act.wait_ge(norm2_ready, 1)

                def normalise2(T):
                    A.activation(tile_of(acc, T), tile_of(acc, T), ACT.Identity, bias=shift[:, bass.ds(T, 1)], scale=rstd[:, bass.ds(T, 1)]).then_inc(normed, 1)

                def relu_of(g):
                    act.wait_ge(shifted2, g + 1)
                    act.sem_inc(passed2, 1)
                    A.activation(ks[:, bass.ds(g * NB, NB), 1, :], grp(acc, g), ACT.Relu).then_inc(relu_ready, 1)
                for T in range(2 * NB):
                    normalise2(T)
                with act.Fori(0, NG - 2) as g:
                    for n in range(NB):
                        normalise2(g * NB + (2 * NB + n))
                    relu_of(g)
                relu_of(NG - 2)
                relu_of(NG - 1)
                act.wait_ge(var_ready, 2)
                A.sqrt(t_a[:, :], t_b[:, :]).then_inc(root_ready, 1)
                act.wait_ge(norm2_ready, 2)
                with act.Fori(0, BY_ACT * NB) as T:
                    A.activation(skip_of(T), tile_of(xs, T), ACT.Relu, bias=shift[:, bass.ds(T, 1)], scale=rstd[:, bass.ds(T, 1)]).then_inc(h2_ready, 1)

            @block.sync
            def _(sp):
                def store(g):
                    sp.dma_start(h_tab[bass.ds(g * (NB * P), NB * P), :].rearrange("(t p) d -> p t d", p=P), ks[:, bass.ds(g * NB, NB), 1, :]).then_inc(h2_stored, 16)
                with sp.Fori(0, BY_ACT) as g:
                    sp.wait_ge(h2_ready, g * NB + NB)
                    store(g)
                with sp.Fori(BY_ACT, NG) as g:
                    sp.wait_ge(h2_max, g - (BY_ACT - 1))
                    store(g)
                sp.wait_ge(h2_stored, 16 * NG)

        stage.close()
        h_ring = tb("h_ring", [P, U, D])
        hot = tb("hot2", [P, U, P])
        own = tb("own", [P, D])
        ownT = tb("ownT", [P, 2, P])
        with nc.Block() as block:
            sums_done, sums_added, hot_ready = sem("n_sums_done"), sem("n_sums_added"), sem("n_hot_ready")
            got, pool_part, index_first, index_next = gather_rows("h", h_tab, lambda u: h_ring[:, u, :], lambda u: [(sums_done, U, u + 1)])

            @block.gpsimd
            def _(pool):
                pool_part(pool)

            own_read, own_turned, own_copied, own_done, own_added = [sem("own_" + n) for n in "read turned copied done added".split()]

            @block.scalar
            def _(act):
                def read_own(T, k):
                    act.wait_ge(own_turned, k + 1)
                    A.copy(own[:, :], ks[:, bass.ds(T, 1), 1, :].rearrange("p o d -> p (o d)")).then_inc(own_read, 1)

                def copy_own(k):
                    act.wait_ge(own_turned, k + 2)
                    A.copy(ownT[:, :, :].rearrange("p c n -> p (c n)"), bank[4][:, 0:2 * P]).then_inc(own_copied, 1)
                index_first(act)
                act.sem_inc(own_turned, 1)
                for k in range(LEFT):
                    read_own(ITERS + k, k)
                    copy_own(k)
                with act.Fori(0, ITERS) as i:
                    read_own(i, i + LEFT)
                    index_next(act, i, lambda: copy_own(i + LEFT))

            @block.tensor
            def _(pe):
                def turn_own(k):
                    pe.wait_ge(own_read, k + 1)
                    for c in range(2):
                        last = T_.transpose(bank[4][:, c * P:(c + 1) * P], own[:, c * P:(c + 1) * P], ident[:, :])
                    last.then_inc(own_turned, 1)

                def multiply_own(k):
                    pe.wait_ge(own_copied, k + 1)
                    pe.wait_ge(own_added, k + 1)
                    for c in range(2):
                        last = T_.matmul(bank[5][:, 0:D], ownT[:, c, :], w1T[:, 2 + c, :], start=(c == 0), stop=(c == 1))
                    last.then_inc(own_done, 1)
                pe.sem_inc(sums_done, U)
                for k in range(LEFT):
                    turn_own(k)
                    multiply_own(k)
                with pe.Fori(0, ITERS) as i:
                    for u in range(U):
                        if u == U // 4:
                            turn_own(i + LEFT)
                        if u == U - Q:
                            multiply_own(i + LEFT)
                        if u % Q == 0:
                            pe.wait_ge(hot_ready, i * NQ + (u // Q + 1))
                        pe.wait_ge(got[u], i * 16 + 16)
                        pe.wait_ge(sums_added, i * U + (u + 1))
                        T_.matmul(bank[u % 4][:, 0:D], hot[:, u, :], h_ring[:, u, :], start=True, stop=True).then_inc(sums_done, 1)

            @block.vector
            def _(dve):
                f = Chain(dve, "neighbour_chain").follow
                dve.sem_inc(sums_added, 4)
                dve.sem_inc(own_added, 1)

                def add_own(T, k):
                    dve.wait_ge(own_done, k + 1)
                    row = xs[:, bass.ds(T, 1), :].rearrange("p o d -> p (o d)")
                    V.tensor_tensor(row, row, bank[5][:, 0:D], ALU.add).then_inc(own_added, 1)

                def build(u, t):
                    return V.tensor_scalar(hot[:, u, :], iota_f[:, 0:P], v_loc[:, t], v_wgt[:, t], ALU.is_equal, ALU.mult)
                for u in range(Q):
                    last = build(u, slice(u, u + 1))
                last.then_inc(hot_ready, 1)
                f(V.tensor_tensor(xs[:, :, :], xs[:, :, :], b1s[:, :].unsqueeze(1).to_broadcast([P, NT, D]), ALU.add))
                for k in range(LEFT):
                    add_own(ITERS + k, k)
                with dve.Fori(0, ITERS) as i:
                    tiles = load_node_tiles(dve, i)
                    for u in range(U):
                        last = build((u + Q) % U, bass.ds(i * U + (u + Q), 1))
                        if u % Q == Q - 1:
                            last.then_inc(hot_ready, 1)
                        dve.wait_ge(sums_done, i * U + (U + u + 1))
                        dve.wait_ge(sums_added, i * U + (4 + u))
                        a = acc_odd[:, bass.ds(tiles[u], 1), 0:D].rearrange("p o d -> p (o d)")
                        V.tensor_tensor(a, a, bank[u % 4][:, 0:D], ALU.add).then_inc(sums_added, 1)
                    add_own(i, i + LEFT)

        stage.close()
        h_buf = tb("mean_buf", [P, NB, D])
        hT = tb("mean_T", [P, NB, 2, P])
        with nc.Block() as block:
            mean_ready, turned, meanT_ready, out_done, out_ready = [sem("f_" + n) for n in "mean turned meanT out_done out_ready".split()]
            stored = sem("stored")
            turn_bank = [bank[2 if n == NB - 1 else n % 2][:, 0:D] for n in range(NB)]
            out_bank = [bank[3 + n][:, 0:D] for n in range(NB)]
            assert 3 + NB <= 8 and 2 * P == D

            def tiles_of(eng, body):
                with eng.Fori(0, NG - 1) as g:
                    for n in range(NB):
                        body(g * NB + n, n, False)
                for n in range(NB):
                    body((NG - 1) * NB + n, n, True)

            @block.vector
            def _(dve):
                def mean_of(T, n):
                    V.tensor_scalar(h_buf[:, n, :], acc_odd[:, bass.ds(T, 1), 0:D].rearrange("p o d -> p (o d)"), rdeg[:, bass.ds(T, 1)], None,
                                    ALU.mult).then_inc(mean_ready, 1)
                for T in range(3):
                    mean_of(T, T)

                def body(T, n, last):
                    if not last or n + 3 < NB:
                        mean_of(T + 3, (n + 3) % NB)
                    dve.wait_ge(out_done, T + 1)
                    row = xs[:, bass.ds(T, 1), :].rearrange("p o d -> p (o d)")
                    V.tensor_tensor(row, row, out_bank[n], ALU.add).then_inc(out_ready, 1)
                tiles_of(dve, body)

            @block.tensor
            def _(pe):
                def turn(T, n):
                    pe.wait_ge(mean_ready, T + 1)
                    for c in range(2):
                        last = T_.transpose(turn_bank[n][:, c * P:(c + 1) * P], h_buf[:, n, c * P:(c + 1) * P], ident[:, :])
                    last.then_inc(turned, 1)
                turn(0, 0)

                def body(T, n, last):
                    if not last or n + 1 < NB:
                        turn(T + 1, (n + 1) % NB)
                    pe.wait_ge(meanT_ready, T + 1)
                    for c in range(2):
                        mm = T_.matmul(out_bank[n], hT[:, n, c, :], w1T[:, c, :], start=(c == 0), stop=(c == 1))
                    mm.then_inc(out_done, 1)
                tiles_of(pe, body)

            @block.scalar
            def _(act):
                def body(T, n, last):
                    act.wait_ge(turned, T + 1)
                    A.copy(hT[:, n, :, :].rearrange("p c n -> p (c n)"), turn_bank[n]).then_inc(meanT_ready, 1)
                tiles_of(act, body)

            @block.sync
            def _(sp):
                with sp.Fori(0, NT - 1) as T:
                    sp.wait_ge(out_ready, T + 1)
                    sp.dma_start(out[bass.ds(T * P, P), :], xs[:, bass.ds(T, 1), :].rearrange("p o d -> p (o d)")).then_inc(stored, 16)
                sp.wait_ge(out_ready, NT)
                sp.dma_start(out[(NT - 1) * P:N, :], xs[0:LAST_ROWS, NT - 1, :]).then_inc(stored, 16)
                sp.wait_ge(stored, 16 * NT)
        stage.close()


_INS = ['x', 'src', 'dst', 'edge_weight1', 'L0_gnn_Wq', 'L0_gnn_bq', 'L0_gnn_Wk', 'L0_gnn_bk', 'L0_gnn_Wv', 'L0_gnn_bv',
        'L0_gnn_Wskip', 'L0_gnn_bskip', 'L0_gnn_Wgate', 'L0_gnn_bgate', 'L0_gnn_ln_w', 'L0_gnn_ln_b',
        'L0_gnn_prelu_a', 'L1_gnn_W', 'L1_gnn_b']
_OUTS = [((3125, 256), 'float32')]


def kernel(**inputs):
    import numpy as _np
    import concourse.bacc as _bacc
    from concourse import mybir as _mybir
    from concourse.bass_utils import run_bass_kernel_spmd as _run

    nc = _bacc.Bacc("TRN2", target_bir_lowering=False, num_devices=1)
    arrays, args = {}, []
    for name in _INS:
        a = _np.ascontiguousarray(inputs[name])
        if a.ndim == 0:
            a = a.reshape(1)
        arrays[f"in_{name}_dram"] = a
        args.append(nc.dram_tensor(f"in_{name}_dram", a.shape, _mybir.dt.from_np(a.dtype), kind="ExternalInput").ap())
    for i, (shape, dtype) in enumerate(_OUTS):
        dt = _mybir.dt.from_np(_np.dtype(dtype))
        args.append(nc.dram_tensor(f"out_{i}_dram", shape, dt, kind="ExternalOutput").ap())
    gnn_kernel(nc, *args)
    r = _run(nc, [arrays], core_ids=[0])
    got = tuple(r.results[0][f"out_{i}_dram"] for i in range(len(_OUTS)))
    return got[0]
```
